# Optimizing a Trainium2 kernel written in Bass

```python
import numpy as np
import jax
import jax.numpy as jnp

def _softmax(x, axis=-1):
    return jax.nn.softmax(x, axis=axis)

def _gelu(x):
    return jax.nn.gelu(x, approximate=True)

def _silu(x):
    return jax.nn.silu(x)

def _sigmoid(x):
    return jax.nn.sigmoid(x)

def _layernorm(x, axis=-1, eps=1e-05):
    m = jnp.mean(x, axis=axis, keepdims=True)
    v = jnp.var(x, axis=axis, keepdims=True)
    return (x - m) / jnp.sqrt(v + eps)

def _scatter_add(tgt, idx, src, axis=0):
    return tgt.at[idx].add(src)

def _segment_sum(src, seg, n):
    return jax.ops.segment_sum(src, seg, n)
kernel_name = 'mk_adj_resnorm_d2_adj_r2_b83687'

def setup_inputs(seed: int=0):
    np.random.seed(seed)
    _w = jnp.asarray

    def _rec_inputs():
        import jax
        import jax.numpy as jnp
        _gk = jax.random.key(seed)
        x = 7.22e-05 + 1 * jax.random.normal(jax.random.fold_in(_gk, 1), (16, 512, 128), jnp.float32)
        _w = (1.0 + jnp.arange(512, dtype=jnp.float32)) ** (-0.5)
        _w = _w / _w.mean()
        _pij = jnp.clip(0.00390625 * _w[:, None] * _w[None, :], 0.0, 1.0)
        _a = jax.random.uniform(jax.random.fold_in(_gk, 2), (16, 512, 512)) < _pij
        _a = jnp.logical_or(_a, jnp.swapaxes(_a, -1, -2))
        _a = jnp.logical_or(_a, jnp.eye(512, dtype=bool))
        _af = _a.astype(jnp.float32)
        adj = _af
        return (x, adj)
    x, adj = _rec_inputs()

    def _L0_gnn_setup():
        import jax, jax.numpy as jnp
        import numpy as np
        from jax import lax
        DIM = 128
        EPS = 1e-05

        def _bn(h, g, b, m, v):
            scale = g / jnp.sqrt(v + EPS)
            return h * scale[None, :, None] + (b - m * scale)[None, :, None]

        def _conv1d(h, w, pad):
            return lax.conv_general_dilated(h, w, window_strides=(1,), padding=[(pad, pad)], dimension_numbers=('NCH', 'OIH', 'NCH'))
        key = jax.random.key(seed)
        ks = jax.random.split(key, 16)
        bs, n, d = (16, 1024, DIM)
        s = 0.05
        return {'x': jax.random.normal(ks[0], (bs, n, d), jnp.float32), 'mask': jnp.ones((bs, n, n), jnp.float32), 'w_se': jax.random.normal(ks[1], (3, d), jnp.float32) * s, 'b_se': jnp.zeros((3,), jnp.float32), 'conv1_w': jax.random.normal(ks[2], (d, d, 1), jnp.float32) * s, 'bn1_g': jnp.ones((d,), jnp.float32), 'bn1_b': jnp.zeros((d,), jnp.float32), 'bn1_m': jnp.zeros((d,), jnp.float32), 'bn1_v': jnp.ones((d,), jnp.float32), 'conv2_w': jax.random.normal(ks[3], (d, d, 17), jnp.float32) * s, 'bn2_g': jnp.ones((d,), jnp.float32), 'bn2_b': jnp.zeros((d,), jnp.float32), 'bn2_m': jnp.zeros((d,), jnp.float32), 'bn2_v': jnp.ones((d,), jnp.float32), 'w_msg': jax.random.normal(ks[4], (d, d), jnp.float32) * s, 'b_msg': jnp.zeros((d,), jnp.float32), 'w_ih': jax.random.normal(ks[5], (3 * d, 2 * d), jnp.float32) * s, 'b_ih': jnp.zeros((3 * d,), jnp.float32), 'w_hh': jax.random.normal(ks[6], (3 * d, d), jnp.float32) * s, 'b_hh': jnp.zeros((3 * d,), jnp.float32)}
    _L0_gnn_all = _L0_gnn_setup()
    _L0_gnn_in = {k: v for k, v in _L0_gnn_all.items() if k in ('w_se', 'b_se', 'conv1_w', 'bn1_g', 'bn1_b', 'bn1_m', 'bn1_v', 'conv2_w', 'bn2_g', 'bn2_b', 'bn2_m', 'bn2_v', 'w_msg', 'b_msg', 'w_ih', 'b_ih', 'w_hh', 'b_hh')}
    del _L0_gnn_all

    def _L1_gnn_setup():
        import jax, jax.numpy as jnp
        import numpy as np
        B, N, IN_F, OUT_F = (2, 2048, 128, 128)
        ALPHA = 0.2
        MASK_NEG = -9000000000000000.0
        SINK_NEG = -1000000000.0
        key = jax.random.key(seed)
        kx, kadj, kw, kbw, kai, kbi, kaj, kbj = jax.random.split(key, 8)
        x = jax.random.normal(kx, (B, N, IN_F), dtype=jnp.float32)
        adjs = (jax.random.uniform(kadj, (B, N, N)) < 0.01).astype(jnp.float32)

        def xavier(k, shape, gain=1.414):
            fan_out, fan_in = shape
            bound = gain * np.sqrt(6.0 / (fan_in + fan_out))
            return jax.random.uniform(k, shape, minval=-bound, maxval=bound, dtype=jnp.float32)
        W = xavier(kw, (OUT_F, IN_F))
        bW = jax.random.uniform(kbw, (OUT_F,), minval=-1 / np.sqrt(IN_F), maxval=1 / np.sqrt(IN_F), dtype=jnp.float32)
        wai = xavier(kai, (1, OUT_F))
        bai = jax.random.uniform(kbi, (1,), minval=-1 / np.sqrt(OUT_F), maxval=1 / np.sqrt(OUT_F), dtype=jnp.float32)
        waj = xavier(kaj, (1, OUT_F))
        baj = jax.random.uniform(kbj, (1,), minval=-1 / np.sqrt(OUT_F), maxval=1 / np.sqrt(OUT_F), dtype=jnp.float32)
        return {'x': x, 'adjs': adjs, 'W': W, 'bW': bW, 'wai': wai, 'bai': bai, 'waj': waj, 'baj': baj}
    _L1_gnn_all = _L1_gnn_setup()
    _L1_gnn_in = {k: v for k, v in _L1_gnn_all.items() if k in ('W', 'bW', 'wai', 'bai', 'waj', 'baj')}
    del _L1_gnn_all
    return {'x': x, 'adj': adj, 'L0_gnn_w_se': _L0_gnn_in['w_se'], 'L0_gnn_b_se': _L0_gnn_in['b_se'], 'L0_gnn_conv1_w': _L0_gnn_in['conv1_w'], 'L0_gnn_bn1_g': _L0_gnn_in['bn1_g'], 'L0_gnn_bn1_b': _L0_gnn_in['bn1_b'], 'L0_gnn_bn1_m': _L0_gnn_in['bn1_m'], 'L0_gnn_bn1_v': _L0_gnn_in['bn1_v'], 'L0_gnn_conv2_w': _L0_gnn_in['conv2_w'], 'L0_gnn_bn2_g': _L0_gnn_in['bn2_g'], 'L0_gnn_bn2_b': _L0_gnn_in['bn2_b'], 'L0_gnn_bn2_m': _L0_gnn_in['bn2_m'], 'L0_gnn_bn2_v': _L0_gnn_in['bn2_v'], 'L0_gnn_w_msg': _L0_gnn_in['w_msg'], 'L0_gnn_b_msg': _L0_gnn_in['b_msg'], 'L0_gnn_w_ih': _L0_gnn_in['w_ih'], 'L0_gnn_b_ih': _L0_gnn_in['b_ih'], 'L0_gnn_w_hh': _L0_gnn_in['w_hh'], 'L0_gnn_b_hh': _L0_gnn_in['b_hh'], 'L1_gnn_W': _L1_gnn_in['W'], 'L1_gnn_bW': _L1_gnn_in['bW'], 'L1_gnn_wai': _L1_gnn_in['wai'], 'L1_gnn_bai': _L1_gnn_in['bai'], 'L1_gnn_waj': _L1_gnn_in['waj'], 'L1_gnn_baj': _L1_gnn_in['baj']}

def reference(x, adj, L0_gnn_w_se, L0_gnn_b_se, L0_gnn_conv1_w, L0_gnn_bn1_g, L0_gnn_bn1_b, L0_gnn_bn1_m, L0_gnn_bn1_v, L0_gnn_conv2_w, L0_gnn_bn2_g, L0_gnn_bn2_b, L0_gnn_bn2_m, L0_gnn_bn2_v, L0_gnn_w_msg, L0_gnn_b_msg, L0_gnn_w_ih, L0_gnn_b_ih, L0_gnn_w_hh, L0_gnn_b_hh, L1_gnn_W, L1_gnn_bW, L1_gnn_wai, L1_gnn_bai, L1_gnn_waj, L1_gnn_baj):
    import jax
    import jax.numpy as jnp

    def _L0_gnn_ref(x, mask, w_se, b_se, conv1_w, bn1_g, bn1_b, bn1_m, bn1_v, conv2_w, bn2_g, bn2_b, bn2_m, bn2_v, w_msg, b_msg, w_ih, b_ih, w_hh, b_hh):
        import jax, jax.numpy as jnp
        import numpy as np
        from jax import lax
        DIM = 128
        EPS = 1e-05

        def _bn(h, g, b, m, v):
            scale = g / jnp.sqrt(v + EPS)
            return h * scale[None, :, None] + (b - m * scale)[None, :, None]

        def _conv1d(h, w, pad):
            return lax.conv_general_dilated(h, w, window_strides=(1,), padding=[(pad, pad)], dimension_numbers=('NCH', 'OIH', 'NCH'))
        d = x.shape[-1]
        xc = jnp.transpose(x, (0, 2, 1))
        h = _bn(_conv1d(xc, conv1_w, 0), bn1_g, bn1_b, bn1_m, bn1_v)
        h = jax.nn.relu(h)
        h = _bn(_conv1d(h, conv2_w, 8), bn2_g, bn2_b, bn2_m, bn2_v)
        x_conv = jnp.transpose(jax.nn.relu(h + xc), (0, 2, 1))
        s = x @ w_se.T + b_se
        sq = jnp.sum(s * s, axis=-1)
        dist = sq[:, :, None] + sq[:, None, :] - 2.0 * jnp.einsum('bnd,bmd->bnm', s, s)
        A = jnp.exp(-dist) * mask
        msg = jax.nn.relu(x @ w_msg.T + b_msg)
        x_nmp = jnp.einsum('bnm,bmd->bnd', A, msg)
        x_in = jnp.concatenate([x_conv, x_nmp], axis=-1)
        gi = x_in @ w_ih.T + b_ih
        gh = x @ w_hh.T + b_hh
        gi_r, gi_z, gi_n = (gi[..., :d], gi[..., d:2 * d], gi[..., 2 * d:])
        gh_r, gh_z, gh_n = (gh[..., :d], gh[..., d:2 * d], gh[..., 2 * d:])
        r = jax.nn.sigmoid(gi_r + gh_r)
        z = jax.nn.sigmoid(gi_z + gh_z)
        nn_ = jnp.tanh(gi_n + r * gh_n)
        return (1.0 - z) * nn_ + z * x

    def _L1_gnn_ref(x, adjs, W, bW, wai, bai, waj, baj):
        import jax, jax.numpy as jnp
        import numpy as np
        B, N, IN_F, OUT_F = (2, 2048, 128, 128)
        ALPHA = 0.2
        MASK_NEG = -9000000000000000.0
        SINK_NEG = -1000000000.0
        b, n, _ = adjs.shape
        z = jnp.einsum('bni,oi->bno', x, W) + bW
        ai = jnp.einsum('bno,ko->bnk', z, wai) + bai
        aj = jnp.einsum('bno,ko->bnk', z, waj) + baj
        e = ai + jnp.swapaxes(aj, 1, 2)
        e = jnp.where(e >= 0, e, ALPHA * e)
        att = jnp.where(adjs > 0, e, MASK_NEG)
        sink = jnp.full((b, n, 1), SINK_NEG, dtype=att.dtype)
        att = jax.nn.softmax(jnp.concatenate([att, sink], axis=-1), axis=-1)[:, :, :n]
        return jnp.einsum('bnm,bmo->bno', att, z)
    x = _layernorm(x + _L0_gnn_ref(x, adj, L0_gnn_w_se, L0_gnn_b_se, L0_gnn_conv1_w, L0_gnn_bn1_g, L0_gnn_bn1_b, L0_gnn_bn1_m, L0_gnn_bn1_v, L0_gnn_conv2_w, L0_gnn_bn2_g, L0_gnn_bn2_b, L0_gnn_bn2_m, L0_gnn_bn2_v, L0_gnn_w_msg, L0_gnn_b_msg, L0_gnn_w_ih, L0_gnn_b_ih, L0_gnn_w_hh, L0_gnn_b_hh), axis=-1)
    x = _layernorm(x + _L1_gnn_ref(x, adj, L1_gnn_W, L1_gnn_bW, L1_gnn_wai, L1_gnn_bai, L1_gnn_waj, L1_gnn_baj), axis=-1)
    return x

_drawn_inputs = setup_inputs


def setup_inputs(seed=0):
    import zlib

    import numpy as np

    out = dict(_drawn_inputs(seed))
    spreads = {'L0_gnn_b_se': (0.0, 0.8),
     'L0_gnn_bn1_g': (1.0, 0.6),
     'L0_gnn_bn1_b': (0.0, 0.371),
     'L0_gnn_bn1_m': (0.0, 0.333),
     'L0_gnn_bn1_v': (1.0, 0.6),
     'L0_gnn_bn2_g': (1.0, 0.2),
     'L0_gnn_bn2_b': (0.0, 0.538),
     'L0_gnn_bn2_m': (0.0, 0.496),
     'L0_gnn_bn2_v': (1.0, 0.6),
     'L0_gnn_b_msg': (0.0, 0.1),
     'L0_gnn_b_ih': (0.0, 0.1),
     'L0_gnn_b_hh': (0.0, 0.281)}
    factors = {}
    for name, (base, spread) in spreads.items():
        noise = np.random.default_rng([zlib.crc32(name.encode()), seed]).standard_normal(out[name].shape)
        drawn = base * np.exp(spread * noise) if base else spread * noise
        out[name] = jnp.asarray(drawn.astype(out[name].dtype))
    for name, factor in factors.items():
        out[name] = (out[name] * factor).astype(out[name].dtype)
    return out
```

```python
import concourse.bass as bass
from concourse import mybir
from contextlib import ExitStack

F32 = mybir.dt.float32
F32R = mybir.dt.float32r
ALU = mybir.AluOpType
ACT = mybir.ActivationFunctionType


class Turn:

    def __init__(self, parity, before, prev, now, loaded, stored, layer0=True, layer1=True,
                 final=True, first0=False, first1=False):
        self.parity = parity
        self.now = now
        self.prev = prev
        self.before = before
        self.loaded = loaded
        self.stored = stored
        self.layer0, self.layer1, self.final = layer0, layer1, final
        self.first0 = first0
        self.first1 = first1


def resnorm_kernel(nc, x, adj, w_se, b_se, conv1_w, bn1_g, bn1_b, bn1_m, bn1_v, conv2_w, bn2_g,
                   bn2_b, bn2_m, bn2_v, w_msg, b_msg, w_ih, b_ih, w_hh, b_hh, W, bW, wai, bai,
                   waj, baj, out):
    G, N, D = x.shape
    P = 128
    C = N // P
    TAPS = conv2_w.shape[2]
    PAD = TAPS // 2
    SE = w_se.shape[0]
    AUG = D + 4
    KU = 4 * SE + 4
    VOFF = 32
    EPS = 1e-5
    ALPHA = 0.2
    SINK = -1e9
    MASKED = -9e15 / ALPHA

    ctx = ExitStack()
    with ctx:
        def sb(name, shape, dt=F32):
            return ctx.enter_context(nc.sbuf_tensor(name, shape, dt))

        def sem(name):
            return ctx.enter_context(nc.semaphore(name))

        ctx.enter_context(nc.allow_non_contiguous_dma("parameter vectors as columns, once"))

        ident = sb("ident", [P, P])
        half_power = sb("half_power", [P, C])
        raw_conv1 = sb("raw_conv1", [P, D])
        raw_conv2 = sb("raw_conv2", [P, D * TAPS])
        raw_msg = sb("raw_msg", [P, D])
        raw_se = sb("raw_se", [SE, D])
        raw_ih = sb("raw_ih", [P, 3, 2 * D])
        raw_hh = sb("raw_hh", [P, 3, D])
        raw_W = sb("raw_W", [P, D])
        NW = 1 + TAPS + 9
        wh = sb("wh", [P, NW, D], F32R)
        wl = sb("wl", [P, NW, D], F32R)
        CONV1, CONV2, IH_CONV, IH_MSG, HH = 0, 1, 1 + TAPS, 4 + TAPS, 7 + TAPS
        msg_wh = sb("msg_wh", [P, AUG], F32R)
        msg_wl = sb("msg_wl", [P, AUG], F32R)
        z_wh = sb("z_wh", [P, AUG], F32R)
        z_wl = sb("z_wl", [P, AUG], F32R)
        aug_full = sb("aug_full", [P, 2, AUG])
        bn = sb("bn", [P, 8])
        bn_scale = sb("bn_scale", [P, 2])
        bn_shift = sb("bn_shift", [P, 2])
        bn_tmp = sb("bn_tmp", [P, 2])
        gru_bi = sb("gru_bi", [P, 3])
        gru_bh = sb("gru_bh", [P, 3])
        gru_half = sb("gru_half", [P, 3])
        msg_bias = sb("msg_bias", [P, AUG])
        z_bias = sb("z_bias", [P, AUG])
        att_w = sb("att_w", [P, 2])
        bW_col = sb("bW_col", [P, 1])
        att_b = sb("att_b", [P, 2])

        x_in = sb("x_in", [P, C, D])
        adj_in = sb("adj_in", [P, C, N])
        xT = sb("xT", [P, 2, N])
        xh, xl = sb("xh", [P, N], F32R), sb("xl", [P, N], F32R)
        h1 = sb("h1", [P, N])
        hh, hl = sb("hh", [P, N + 2 * PAD], F32R), sb("hl", [P, N + 2 * PAD], F32R)
        msg_raw = sb("msg_raw", [P, C, AUG])
        msg = sb("msg", [P, C, D])
        s_sq = sb("s_sq", [P, C, SE])
        sq_a, sq_b = sb("sq_a", [P, C, 1]), sb("sq_b", [P, C, 1])
        uv = sb("uv", [P, C, VOFF + KU])
        U, V = sb("U", [KU, N], F32R), sb("V", [KU, N], F32R)
        E = sb("E", [P, 2, N])
        AT = sb("AT", [P, C, N])
        conv_sum = sb("conv_sum", [P, N])
        xc = sb("xc", [P, N])
        xch, xcl = sb("xch", [P, N], F32R), sb("xcl", [P, N], F32R)
        xnh, xnl = sb("xnh", [P, N], F32R), sb("xnl", [P, N], F32R)
        tr, tz, ghb = sb("tr", [P, N]), sb("tz", [P, N]), sb("ghb", [P, N])
        q1, q2, nn = sb("q1", [P, N]), sb("q2", [P, N]), sb("nn", [P, N])
        x_part, n_part, y = sb("x_part", [P, N]), sb("n_part", [P, N]), sb("y", [P, N])
        stats = sb("stats", [P, C, 6])
        mv = sb("mv", [P, C, 2])
        var_eps, rstd = sb("var_eps", [P, C]), sb("rstd", [P, C])
        x1 = sb("x1", [P, C, D])
        x1h, x1l = sb("x1h", [P, N], F32R), sb("x1l", [P, N], F32R)
        z = sb("z", [P, C, AUG])
        AJ, AI = D, D + 1
        no_edge = sb("no_edge", [P, C, N])
        ajm = sb("ajm", [P, C, N])
        amax, u_max, leaky_max = sb("amax", [P, C]), sb("u_max", [P, C]), sb("leaky_max", [P, C])
        neg_max, sink_in, sink = sb("neg_max", [P, C]), sb("sink_in", [P, C]), sb("sink", [P, C])
        ai_small = sb("ai_small", [P, C])
        e_small = sb("e_small", [P, C, N])
        e = sb("e", [P, C, N])
        p = sb("p", [P, C, N])
        row_sum, den, rden = sb("row_sum", [P, C]), sb("den", [P, C]), sb("rden", [P, C])
        pT = sb("pT", [P, C, N])
        oT = sb("oT", [P, N])
        y2 = sb("y2", [P, C, D])
        stats2, mv2 = sb("stats2", [P, C, 6]), sb("mv2", [P, C, 2])
        var_eps2, rstd2 = sb("var_eps2", [P, C]), sb("rstd2", [P, C])
        out_sb = sb("out_sb", [P, C, D])

        bank = [ctx.enter_context(nc.psum_tensor(f"bank{k}", [P, N], F32)) for k in range(8)]
        B_CONV = B_R = bank[0]
        B_Z, B_IN, B_HN = bank[1], bank[2], bank[3]
        B_A, B_B = bank[4], bank[5]
        B_C, B_D = bank[6], bank[7]

        def chunk(ap, c, width=P):
            return ap[:, c * width:(c + 1) * width]

        def pair(b):
            return b[:, 0:2 * AUG].rearrange("p (c f) -> p c f", c=2)

        params_loaded, weights_loaded = sem("params_loaded"), sem("weights_loaded")
        ident_zero, constants_ready = sem("ident_zero"), sem("constants_ready")
        w_turned, w_split, w_high = sem("w_turned"), sem("w_split"), sem("w_high")
        att_folded, aug_copied = sem("att_folded"), sem("aug_copied")
        setup_dve, setup_pow = sem("setup_dve"), sem("setup_pow")
        params_ready = sem("params_ready")
        x_loaded, adj_loaded, out_free = sem("x_loaded"), sem("adj_loaded"), sem("out_free")
        s = {n: sem(n) for n in (
            "xT_mm xT_done xh_done xl_done conv1_mm h1_done hh_done hl_done "
            "msg_mm0 msg_mm1 msg_raw0 msg_raw1 msg_done "
            "uv_sh uv_sl uv_squares uv_sum1 uv_sum uv_sqh uv_sql uv_done uv_mm U_done V_done "
            "dist_mm0 dist_mm1 dist_mm2 dist_mm3 adjT_mm0 adjT_mm1 adjT_mm2 adjT_mm3 "
            "E_done0 E_done1 E_done2 E_done3 AT_done0 AT_done1 AT_done2 AT_done3 "
            "no_edge_done conv2_mm conv_sum_done xc_done xch_done xcl_done nmp_mm xnh_done xnl_done "
            "hn_mm xgates_mm conv_gates_mm gates_mm ghb_done tr_done tz_done q1_done q2_done "
            "nn_done x_part_done n_part_done y_done "
            "yT_mm stats_done mv_done var_done rstd_done x1_done x1T_mm x1h_done x1l_done "
            "z_mm0 z_mm1 z_done0 z_done1 ajb_mm ai_small_done "
            "ajm_done0 ajm_done1 ajm_done2 ajm_done3 u_max_done leaky_max_done neg_max_done "
            "sink_in_done sink_done e_small0 e_small1 e_small2 e_small3 e_done0 e_done1 e_done2 "
            "e_done3 p_done0 p_done1 p_done2 p_done3 pT_mm0 pT_mm1 pT_mm2 pT_mm3 "
            "pT_done0 pT_done1 pT_done2 pT_done3 att_mm oT_done o_mm den_done rden_done "
            "y2_done stats2_done mv2_done var2_done rstd2_done out_done").split()}

        x_dram = x.rearrange("g (c p) d -> g p c d", p=P)
        adj_dram = adj.rearrange("g (c p) m -> g p c m", p=P)
        out_dram = out.rearrange("g (c p) d -> g p c d", p=P)

        def column(v):
            return v.rearrange("(p a) -> p a", a=1)

        def row_everywhere(v):
            return v.rearrange("(a n) -> a n", a=1).to_broadcast([P, v.shape[0]])

        def run_turns(eng, turn):
            turn(Turn(0, None, None, 1, 16, None, layer1=False, final=False, first0=True))
            turn(Turn(1, None, 1, 2, 32, None, final=False, first1=True))
            regs = {}
            for name in ("gm1", "g0", "g1", "g2", "s0", "s1", "s2", "s3"):
                regs[name] = eng.alloc_register(name)
            with eng.Fori(2, G, 2) as g:
                for k, name in enumerate(("gm1", "g0", "g1", "g2")):
                    eng.reg_add(regs[name], g, k - 1)
                for k in range(4):
                    eng.reg_mul(regs[f"s{k}"], regs[("gm1", "g0", "g1", "g2")[k]], 16)
                v = {name: eng.snap(r, min_val=1) for name, r in regs.items()}
                turn(Turn(0, v["gm1"], v["g0"], v["g1"], v["s2"], v["s0"]))
                turn(Turn(1, v["g0"], v["g1"], v["g2"], v["s3"], v["s1"]))
            turn(Turn(G % 2, G - 1, G, None, None, 16 * (G - 1), layer0=False))
            turn(Turn((G + 1) % 2, G, None, None, None, 16 * G, layer0=False, layer1=False))

        block = ctx.enter_context(nc.Block())

        @block.sync
        def _(sp):
            sp.dma_start(x_in[:], x_dram[0]).then_inc(x_loaded, 16)
            sp.dma_start(raw_conv1[:], conv1_w.rearrange("o i k -> o (i k)")).then_inc(weights_loaded, 16)
            sp.dma_start(raw_conv2[:], conv2_w.rearrange("o i k -> o (i k)")).then_inc(weights_loaded, 16)
            sp.dma_start(raw_msg[:], w_msg).then_inc(weights_loaded, 16)
            sp.dma_start(raw_se[:], w_se).then_inc(weights_loaded, 16)
            sp.dma_start(raw_ih[:], w_ih.rearrange("(a o) i -> o a i", a=3)).then_inc(weights_loaded, 16)
            sp.dma_start(raw_hh[:], w_hh.rearrange("(a o) i -> o a i", a=3)).then_inc(weights_loaded, 16)
            sp.dma_start(raw_W[:], W).then_inc(weights_loaded, 16)
            sp.dma_start(adj_in[:], adj_dram[0]).then_inc(adj_loaded, 16)

            def load_x(g, here):
                sp.wait_ge(s["xT_mm"], here)
                sp.dma_start(x_in[:], x_dram[g]).then_inc(x_loaded, 16)

            def load_adj(g, here):
                sp.wait_ge(s["adjT_mm3"], here)
                sp.wait_ge(s["no_edge_done"], here)
                sp.dma_start(adj_in[:], adj_dram[g]).then_inc(adj_loaded, 16)

            def store(g, here):
                sp.wait_ge(s["out_done"], here)
                sp.dma_start(out_dram[g], out_sb[:]).then_inc(out_free, 16)

            for g in range(2):
                load_x(g + 1, g + 1)
                load_adj(g + 1, g + 1)
            with sp.Fori(2, G - 1) as g:
                load_x(g + 1, g + 1)
                load_adj(g + 1, g + 1)
                store(g - 2, g - 1)
            store(G - 3, G - 2)
            store(G - 2, G - 1)
            store(G - 1, G)
            sp.wait_ge(out_free, 16 * (G + 1))

        @block.gpsimd
        def _(pool):
            pool.memset(ident[:], 0.0).then_inc(ident_zero, 1)
            pool.wait_ge(ident_zero, 1)
            pool.affine_select(out=ident[:], in_=ident[:], compare_op=ALU.not_equal, fill=1.0, base=0,
                               pattern=[[-1, P]], channel_multiplier=1).then_inc(constants_ready, 1)
            pool.memset(half_power[:], -0.5).then_inc(constants_ready, 1)
            pool.memset(hh[:].bitcast(F32), 0.0).then_inc(constants_ready, 1)
            pool.memset(hl[:].bitcast(F32), 0.0).then_inc(constants_ready, 1)
            pool.memset(uv[:], 0.0).then_inc(constants_ready, 1)
            pool.wait_ge(constants_ready, 5)
            pool.memset(uv[:, :, 4 * SE + 2:KU], 1.0).then_inc(constants_ready, 1)
            pool.memset(uv[:, :, VOFF + 4 * SE:VOFF + 4 * SE + 2], -1.0).then_inc(constants_ready, 1)
            pool.wait_ge(setup_dve, 1)
            pool.tensor_tensor(bn_scale[:], bn_tmp[:], half_power[:, 0:2], ALU.pow).then_inc(setup_pow, 1)

            def turn(t):
                if t.layer0:
                    def u_view(a):
                        return uv[:, :, 2 * SE * a:2 * SE * (a + 1)].rearrange("p c (b k) -> p c b k", b=2)

                    def v_view(a):
                        return uv[:, :, VOFF:VOFF + 4 * SE].rearrange("p c (b a k) -> p c b a k", b=2, a=2)[:, :, :, a, :]

                    sv = msg_raw[:, :, D:D + SE]

                    def twice(ap):
                        return ap.rearrange("p c (b k) -> p c b k", b=1).to_broadcast([P, C, 2, SE])

                    uq = uv[:, :, 4 * SE:4 * SE + 1]
                    pool.wait_ge(constants_ready, 7)
                    pool.wait_ge(s["msg_raw1"], t.now)
                    pool.wait_ge(s["msg_raw0"], t.now)
                    if not t.first0:
                        pool.wait_ge(s["uv_mm"], t.prev)
                    pool.tensor_copy(u_view(0).bitcast(F32R), twice(sv)).then_inc(s["uv_sh"], 1)
                    pool.tensor_tensor(s_sq[:], sv, sv, ALU.mult).then_inc(s["uv_squares"], 1)
                    pool.wait_ge(s["uv_sh"], t.now)
                    pool.tensor_tensor(u_view(1).bitcast(F32R), twice(sv), u_view(0),
                                       ALU.subtract).then_inc(s["uv_sl"], 1)
                    pool.wait_ge(s["uv_squares"], t.now)
                    pool.tensor_tensor(sq_a[:], s_sq[:, :, 0:1], s_sq[:, :, 1:2],
                                       ALU.add).then_inc(s["uv_sum1"], 1)
                    pool.wait_ge(constants_ready, 7)
                    pool.wait_ge(s["uv_sl"], t.now)
                    pool.tensor_scalar(v_view(0), u_view(0), 2.0, None, ALU.mult)
                    pool.tensor_scalar(v_view(1), u_view(1), 2.0, None, ALU.mult)
                    pool.wait_ge(s["uv_sum1"], t.now)
                    pool.tensor_tensor(sq_b[:], sq_a[:], s_sq[:, :, 2:3], ALU.add).then_inc(s["uv_sum"], 1)
                    pool.wait_ge(constants_ready, 7)
                    pool.wait_ge(s["uv_sum"], t.now)
                    pool.tensor_copy(uq.bitcast(F32R), sq_b[:]).then_inc(s["uv_sqh"], 1)
                    pool.wait_ge(s["uv_sqh"], t.now)
                    pool.tensor_tensor(uv[:, :, 4 * SE + 1:4 * SE + 2].bitcast(F32R), sq_b[:], uq,
                                       ALU.subtract).then_inc(s["uv_sql"], 1)
                    pool.wait_ge(constants_ready, 7)
                    pool.wait_ge(s["uv_sql"], t.now)
                    pool.tensor_scalar(uv[:, :, VOFF + 4 * SE + 2:VOFF + KU],
                                       uv[:, :, 4 * SE:4 * SE + 2], -1.0, None,
                                       ALU.mult).then_inc(s["uv_done"], 1)
                if t.layer1:
                    pool.wait_ge(s["var_done"], t.prev)
                    pool.tensor_tensor(rstd[:], var_eps[:], half_power[:], ALU.pow).then_inc(s["rstd_done"], 1)
                if t.final:
                    pool.wait_ge(s["var2_done"], t.before)
                    pool.tensor_tensor(rstd2[:], var_eps2[:], half_power[:], ALU.pow).then_inc(s["rstd2_done"], 1)

            run_turns(pool, turn)

        @block.scalar
        def _(act):
            for k, v in enumerate((bn1_g, bn1_b, bn1_m, bn1_v, bn2_g, bn2_b, bn2_m, bn2_v)):
                act.dma_start(bn[:, k:k + 1], column(v)).then_inc(params_loaded, 16)
            act.dma_start(gru_bi[:], b_ih.rearrange("(a p) -> p a", a=3)).then_inc(params_loaded, 16)
            act.dma_start(gru_bh[:], b_hh.rearrange("(a p) -> p a", a=3)).then_inc(params_loaded, 16)
            act.dma_start(msg_bias[:, 0:D], row_everywhere(b_msg)).then_inc(params_loaded, 16)
            act.dma_start(msg_bias[:, D:D + SE], row_everywhere(b_se)).then_inc(params_loaded, 16)
            act.dma_start(z_bias[:, 0:D], row_everywhere(bW)).then_inc(params_loaded, 16)
            act.dma_start(att_w[:, 0:1], waj.rearrange("a p -> p a")).then_inc(params_loaded, 16)
            act.dma_start(att_w[:, 1:2], wai.rearrange("a p -> p a")).then_inc(params_loaded, 16)
            act.dma_start(bW_col[:], column(bW)).then_inc(params_loaded, 16)
            act.dma_start(att_b[:, 0:1], row_everywhere(baj)).then_inc(params_loaded, 16)
            act.dma_start(att_b[:, 1:2], row_everywhere(bai)).then_inc(params_loaded, 16)

            def turn(t):
                par = t.parity

                def exp_dist(c):
                    act.wait_ge(s[f"dist_mm{c}"], t.now)
                    if c >= 2:
                        act.wait_ge(s[f"AT_done{c - 2}"], t.now)
                    elif not t.first0:
                        act.wait_ge(s[f"AT_done{c + 2}"], t.prev)
                    act.activation(E[:, c % 2, :], B_A[:], ACT.Exp).then_inc(s[f"E_done{c}"], 1)

                if t.layer0:
                    act.wait_ge(s["xT_mm"], t.now)
                    if t.layer1 and not t.first1:
                        act.wait_ge(s["x_part_done"], t.before)
                    act.activation(xT[:, par, :], B_A[:], ACT.Copy).then_inc(s["xT_done"], 1)
                    if not t.first0:
                        act.wait_ge(s["xgates_mm"], t.prev)
                        act.wait_ge(s["xl_done"], t.prev)
                    act.activation(xh[:], B_A[:], ACT.Copy).then_inc(s["xh_done"], 1)
                if t.layer1:
                    act.wait_ge(s["hn_mm"], t.prev)
                    act.wait_ge(params_ready, 1)
                    if not t.first1:
                        act.wait_ge(s["q1_done"], t.before)
                    act.activation(ghb[:], B_HN[:], ACT.Identity, bias=gru_half[:, 2:3],
                                   scale=0.5).then_inc(s["ghb_done"], 1)
                if t.layer1:
                    act.wait_ge(s["gates_mm"], t.prev)
                    if not t.first1:
                        act.wait_ge(s["q1_done"], t.before)
                    act.activation(tr[:], B_R[:], ACT.Tanh, bias=gru_half[:, 0:1], scale=0.5).then_inc(s["tr_done"], 1)
                    if not t.first1:
                        act.wait_ge(s["n_part_done"], t.before)
                    act.activation(tz[:], B_Z[:], ACT.Tanh, bias=gru_half[:, 1:2], scale=0.5).then_inc(s["tz_done"], 1)
                if t.layer0:
                    act.wait_ge(s["conv1_mm"], t.now)
                    act.wait_ge(params_ready, 1)
                    if not t.first0:
                        act.wait_ge(s["hl_done"], t.prev)
                    act.activation(h1[:], B_B[:], ACT.Relu, bias=bn_shift[:, 0:1],
                                   scale=bn_scale[:, 0:1]).then_inc(s["h1_done"], 1)
                if t.layer1:
                    act.wait_ge(s["q2_done"], t.prev)
                    if not t.first1:
                        act.wait_ge(s["n_part_done"], t.before)
                    act.activation(nn[:], q2[:], ACT.Tanh, bias=gru_bi[:, 2:3]).then_inc(s["nn_done"], 1)
                if t.layer0:
                    act.wait_ge(s["msg_raw1"], t.now)
                    if not t.first0:
                        act.wait_ge(s["nmp_mm"], t.prev)
                    act.activation(msg[:], msg_raw[:, :, 0:D], ACT.Relu).then_inc(s["msg_done"], 1)
                    act.wait_ge(s["uv_mm"], t.now)
                    if not t.first0:
                        act.wait_ge(s["dist_mm3"], t.prev)
                    act.activation(V[:], B_A[VOFF:VOFF + KU, :], ACT.Copy).then_inc(s["V_done"], 1)
                    exp_dist(0)
                    exp_dist(1)
                if t.layer1:
                    act.wait_ge(s["x1T_mm"], t.prev)
                    if not t.first1:
                        act.wait_ge(s["z_mm1"], t.before)
                    act.activation(x1h[:], B_D[:], ACT.Copy).then_inc(s["x1h_done"], 1)
                if t.layer0:
                    exp_dist(2)
                    exp_dist(3)
                if t.layer1:
                    for c in range(C):
                        act.wait_ge(s[f"ajm_done{c}"], t.prev)
                        if c == 0:
                            act.wait_ge(s["ai_small_done"], t.prev)
                        if not t.first1:
                            act.wait_ge(s[f"e_done{c}"], t.before)
                        act.activation(e_small[:, c, :], ajm[:, c, :], ACT.Identity, bias=ai_small[:, c:c + 1],
                                       scale=ALPHA).then_inc(s[f"e_small{c}"], 1)
                if t.layer0:
                    act.wait_ge(s["conv_sum_done"], t.now)
                    if not t.first0:
                        act.wait_ge(s["xcl_done"], t.prev)
                    act.activation(xc[:], conv_sum[:], ACT.Relu, bias=bn_shift[:, 1:2]).then_inc(s["xc_done"], 1)
                if t.layer1:
                    act.wait_ge(s["sink_in_done"], t.prev)
                    if not t.first1:
                        act.wait_ge(s["den_done"], t.before)
                    act.activation(sink[:], sink_in[:], ACT.Exp).then_inc(s["sink_done"], 1)
                    for c in range(C):
                        act.wait_ge(s[f"e_done{c}"], t.prev)
                        if not t.first1:
                            act.wait_ge(s[f"pT_mm{c}"], t.before)
                            if c == 0:
                                act.wait_ge(s["den_done"], t.before)
                        act.activation(p[:, c, :], e[:, c, :], ACT.Exp, bias=neg_max[:, c:c + 1],
                                       accum_out=row_sum[:, c:c + 1]).then_inc(s[f"p_done{c}"], 1)
                        if t.layer0 and c == 1:
                            act.wait_ge(s["nmp_mm"], t.now)
                            if not t.first0:
                                act.wait_ge(s["gates_mm"], t.prev)
                            act.activation(xnh[:], B_A[:], ACT.Copy).then_inc(s["xnh_done"], 1)
                    for c in (0, 2):
                        act.wait_ge(s[f"pT_mm{c}"], t.prev)
                        if not t.first1:
                            act.wait_ge(s["att_mm"], t.before)
                        act.activation(pT[:, :, c * P:(c + 1) * P],
                                       B_D[:].rearrange("p (m n) -> p m n", m=C),
                                       ACT.Copy).then_inc(s[f"pT_done{c}"], 1)
                    act.wait_ge(s["att_mm"], t.prev)
                    if not t.first1:
                        act.wait_ge(s["o_mm"], t.before)
                    act.activation(oT[:], B_D[:], ACT.Copy).then_inc(s["oT_done"], 1)
                elif t.layer0:
                    act.wait_ge(s["nmp_mm"], t.now)
                    act.activation(xnh[:], B_A[:], ACT.Copy).then_inc(s["xnh_done"], 1)

            act.wait_ge(params_loaded, 18 * 16)
            run_turns(act, turn)

        @block.vector
        def _(dve):
            bn4 = bn[:].rearrange("p (n k) -> p n k", n=2)
            dve.wait_ge(params_loaded, 18 * 16)
            dve.tensor_scalar(bn_tmp[:], bn4[:, :, 3], EPS, None, ALU.add).then_inc(setup_dve, 1)
            dve.memset(msg_bias[:, D + SE:AUG], 0.0).then_inc(out_free, 16)
            dve.memset(z_bias[:, D + 2:AUG], 0.0)
            dve.memset(aug_full[:], 0.0).then_inc(setup_dve, 1)
            dve.tensor_tensor(gru_half[:, 0:2], gru_bi[:, 0:2], gru_bh[:, 0:2], ALU.add)
            dve.tensor_copy(gru_half[:, 2:3], gru_bh[:, 2:3]).then_inc(setup_dve, 1)
            dve.wait_ge(setup_dve, 3)
            dve.tensor_scalar(gru_half[:], gru_half[:], 0.5, None, ALU.mult).then_inc(setup_dve, 1)
            dve.wait_ge(setup_pow, 1)
            dve.tensor_tensor(bn_scale[:], bn_scale[:], bn4[:, :, 0], ALU.mult).then_inc(setup_dve, 1)
            dve.wait_ge(setup_dve, 5)
            dve.tensor_tensor(bn_tmp[:], bn_scale[:], bn4[:, :, 2], ALU.mult).then_inc(setup_dve, 1)
            dve.wait_ge(setup_dve, 6)
            dve.tensor_tensor(bn_shift[:], bn4[:, :, 1], bn_tmp[:], ALU.subtract).then_inc(params_ready, 1)

            blocks = NW
            for k in range(0, blocks, C):
                n = min(C, blocks - k)
                b = bank[(k // C) % 4]
                src = b[:, 0:n * P].rearrange("p (w o) -> p w o", w=n)
                dve.wait_ge(w_turned, k // C + 1)
                dve.tensor_copy(wh[:, k:k + n, :], src).then_inc(w_high, 1)
                dve.wait_ge(w_high, k // C + 1)
                dve.tensor_tensor(wl[:, k:k + n, :], src, wh[:, k:k + n, :].bitcast(F32),
                                  ALU.subtract).then_inc(w_split, 1)
            groups = -(-blocks // C)
            dve.wait_ge(att_folded, 1)
            dve.wait_ge(setup_dve, 2)
            dve.tensor_copy(aug_full[:, 0, 0:D + SE], B_C[:, 0:D + SE]).then_inc(aug_copied, 1)
            dve.tensor_copy(aug_full[:, 1, 0:D + 2], B_C[:, 256:256 + D + 2]).then_inc(aug_copied, 1)
            dve.tensor_tensor(z_bias[:, D:D + 2], B_D[:, 0:2], att_b[:], ALU.add).then_inc(aug_copied, 1)
            dve.wait_ge(aug_copied, 3)
            dve.tensor_copy(msg_wh[:], aug_full[:, 0, :]).then_inc(aug_copied, 1)
            dve.tensor_copy(z_wh[:], aug_full[:, 1, :]).then_inc(aug_copied, 1)
            dve.wait_ge(aug_copied, 5)
            dve.tensor_tensor(msg_wl[:], aug_full[:, 0, :], msg_wh[:].bitcast(F32),
                              ALU.subtract).then_inc(aug_copied, 1)
            dve.tensor_tensor(z_wl[:], aug_full[:, 1, :], z_wh[:].bitcast(F32),
                              ALU.subtract).then_inc(aug_copied, 1)

            def bias_pair(b):
                return b[:].rearrange("p (c f) -> p c f", c=1).to_broadcast([P, 2, AUG])

            def turn(t):
                par = t.parity

                def mask_AT(c):
                    dve.wait_ge(s[f"E_done{c}"], t.now)
                    dve.wait_ge(s[f"adjT_mm{c}"], t.now)
                    if not t.first0:
                        dve.wait_ge(s["nmp_mm"], t.prev)
                    dve.tensor_tensor(AT[:, c, :], E[:, c % 2, :], (B_B, B_IN)[c % 2][:],
                                      ALU.mult).then_inc(s[f"AT_done{c}"], 1)

                if t.layer0:
                    dve.wait_ge(s["xh_done"], t.now)
                    dve.wait_ge(s["xT_done"], t.now)
                    if not t.first0:
                        dve.wait_ge(s["xgates_mm"], t.prev)
                    dve.tensor_tensor(xl[:], xT[:, par, :], xh[:].bitcast(F32),
                                      ALU.subtract).then_inc(s["xl_done"], 1)
                if t.final:
                    if not t.layer1:
                        dve.wait_ge(s["out_done"], G - 1)
                    else:
                        dve.wait_ge(s["no_edge_done"], t.prev)
                    dve.wait_ge(s["rden_done"], t.before)
                    dve.wait_ge(s["o_mm"], t.before)
                    for c in range(C):
                        last = dve.scalar_tensor_tensor(out=y2[:, c, :], in0=chunk(B_C, c), scalar=rden[:, c:c + 1],
                                                        in1=x1[:, c, :], op0=ALU.mult, op1=ALU.add)
                    last.then_inc(s["y2_done"], 1)
                if t.layer0:
                    body = slice(PAD, PAD + N)
                    dve.wait_ge(s["h1_done"], t.now)
                    if t.first0:
                        dve.wait_ge(constants_ready, 4)
                    else:
                        dve.wait_ge(s["conv2_mm"], t.prev)
                    dve.tensor_copy(hh[:, body], h1[:]).then_inc(s["hh_done"], 1)
                    dve.wait_ge(s["hh_done"], t.now)
                    if not t.first0:
                        dve.wait_ge(s["conv2_mm"], t.prev)
                    dve.tensor_tensor(hl[:, body], h1[:], hh[:, body].bitcast(F32),
                                      ALU.subtract).then_inc(s["hl_done"], 1)
                if t.layer1:
                    dve.wait_ge(s["tr_done"], t.prev)
                    dve.wait_ge(s["ghb_done"], t.prev)
                    if not t.first1:
                        dve.wait_ge(s["q2_done"], t.before)
                    dve.scalar_tensor_tensor(out=q1[:], in0=tr[:], scalar=1.0, in1=ghb[:], op0=ALU.add,
                                             op1=ALU.mult).then_inc(s["q1_done"], 1)
                if t.layer1:
                    dve.wait_ge(s["q1_done"], t.prev)
                    if not t.first1:
                        dve.wait_ge(s["nn_done"], t.before)
                    dve.tensor_tensor(q2[:], q1[:], B_IN[:], ALU.add).then_inc(s["q2_done"], 1)
                if t.layer1:
                    dve.wait_ge(s["tz_done"], t.prev)
                    if not t.first1:
                        dve.wait_ge(s["y_done"], t.before)
                    dve.scalar_tensor_tensor(out=x_part[:], in0=tz[:], scalar=3.0, in1=xT[:, 1 - par, :], op0=ALU.add,
                                             op1=ALU.mult).then_inc(s["x_part_done"], 1)
                if t.layer0:
                    for k, b in enumerate((B_A, B_B)):
                        dve.wait_ge(s[f"msg_mm{k}"], t.now)
                        if not t.first0:
                            dve.wait_ge(s["msg_done"], t.prev)
                            dve.wait_ge(s["uv_sl"], t.prev)
                        dve.tensor_tensor(msg_raw[:, 2 * k:2 * k + 2, :], pair(b), bias_pair(msg_bias),
                                          ALU.add).then_inc(s[f"msg_raw{k}"], 1)
                if t.layer1:
                    dve.wait_ge(s["nn_done"], t.prev)
                    dve.wait_ge(s["tz_done"], t.prev)
                    if not t.first1:
                        dve.wait_ge(s["y_done"], t.before)
                    dve.scalar_tensor_tensor(out=n_part[:], in0=tz[:], scalar=-1.0, in1=nn[:], op0=ALU.add,
                                             op1=ALU.mult).then_inc(s["n_part_done"], 1)
                    dve.wait_ge(s["n_part_done"], t.prev)
                    dve.wait_ge(s["x_part_done"], t.prev)
                    if not t.first1:
                        dve.wait_ge(s["yT_mm"], t.before)
                    dve.tensor_tensor(y[:], x_part[:], n_part[:], ALU.subtract).then_inc(s["y_done"], 1)
                if t.layer0:
                    dve.wait_ge(s["uv_mm"], t.now)
                    if not t.first0:
                        dve.wait_ge(s["dist_mm3"], t.prev)
                    dve.tensor_copy(U[:], B_A[0:KU, :]).then_inc(s["U_done"], 1)
                if t.layer1:
                    layer_norm_stats(t.prev, B_C[:], "yT_mm", stats, mv, var_eps, "", 4 * EPS)
                if t.layer0:
                    mask_AT(0)
                if t.layer1:
                    dve.wait_ge(s["rstd_done"], t.prev)
                    if not t.first1:
                        dve.wait_ge(s["y2_done"], t.before)
                    for c in range(C):
                        last = dve.tensor_scalar(x1[:, c, :], chunk(B_C, c), mv[:, c, 0:1], rstd[:, c:c + 1],
                                                 ALU.subtract, ALU.mult)
                    last.then_inc(s["x1_done"], 1)
                if t.layer0:
                    mask_AT(1)
                if t.layer1:
                    dve.wait_ge(s["x1h_done"], t.prev)
                    if not t.first1:
                        dve.wait_ge(s["z_mm1"], t.before)
                    dve.tensor_tensor(x1l[:], B_D[:], x1h[:].bitcast(F32), ALU.subtract).then_inc(s["x1l_done"], 1)
                if t.final:
                    layer_norm_stats(t.before, y2[:].rearrange("p c d -> p (c d)"), "y2_done", stats2, mv2, var_eps2, "2", EPS)
                if t.layer0:
                    mask_AT(2)
                if t.layer1:
                    for k, b in enumerate((B_C, B_D)):
                        dve.wait_ge(s[f"z_mm{k}"], t.prev)
                        if not t.first1:
                            dve.wait_ge(s["att_mm"], t.before)
                            dve.wait_ge(s["e_done3"], t.before)
                            dve.wait_ge(s["u_max_done"], t.before)
                        dve.tensor_tensor(z[:, 2 * k:2 * k + 2, :], pair(b), bias_pair(z_bias),
                                          ALU.add).then_inc(s[f"z_done{k}"], 1)
                    dve.wait_ge(s["z_done1"], t.prev)
                    if not t.first1:
                        dve.wait_ge(s["e_small3"], t.before)
                    dve.tensor_scalar(ai_small[:], z[:, :, AI], ALPHA, None, ALU.mult).then_inc(s["ai_small_done"], 1)
                if t.layer0:
                    mask_AT(3)
                if t.layer1:
                    for c in range(C):
                        dve.wait_ge(constants_ready, 1)
                        dve.wait_ge(s["ajb_mm"], t.prev)
                        dve.wait_ge(s["no_edge_done"], t.prev)
                        if not t.first1:
                            dve.wait_ge(s[f"e_done{c}"], t.before)
                            dve.wait_ge(s[f"e_small{c}"], t.before)
                            dve.wait_ge(s["u_max_done"], t.before)
                        dve.tensor_tensor_reduce(out=ajm[:, c, :], in0=no_edge[:, c, :], in1=B_C[:], scale=1.0,
                                                 scalar=-3.0e38, op0=ALU.add, op1=ALU.max,
                                                 accum_out=amax[:, c:c + 1]).then_inc(s[f"ajm_done{c}"], 1)
                if t.layer0:
                    dve.wait_ge(s["conv2_mm"], t.now)
                    if t.first0:
                        dve.wait_ge(s["xT_done"], t.now)
                    else:
                        dve.wait_ge(s["xc_done"], t.prev)
                    dve.scalar_tensor_tensor(out=conv_sum[:], in0=B_CONV[:], scalar=bn_scale[:, 1:2],
                                             in1=xT[:, par, :], op0=ALU.mult,
                                             op1=ALU.add).then_inc(s["conv_sum_done"], 1)
                if t.layer1:
                    dve.wait_ge(s["ajm_done3"], t.prev)
                    dve.tensor_tensor(u_max[:], amax[:], z[:, :, AI], ALU.add).then_inc(s["u_max_done"], 1)
                    dve.wait_ge(s["u_max_done"], t.prev)
                    dve.scalar_tensor_tensor(out=leaky_max[:], in0=u_max[:], scalar=ALPHA, in1=u_max[:],
                                             op0=ALU.mult, op1=ALU.max).then_inc(s["leaky_max_done"], 1)
                    dve.wait_ge(s["leaky_max_done"], t.prev)
                    if not t.first1:
                        dve.wait_ge(s["p_done3"], t.before)
                    dve.tensor_scalar(neg_max[:], leaky_max[:], SINK, -1.0, ALU.max,
                                      ALU.mult).then_inc(s["neg_max_done"], 1)
                    dve.wait_ge(s["neg_max_done"], t.prev)
                    if not t.first1:
                        dve.wait_ge(s["sink_done"], t.before)
                    dve.tensor_scalar(sink_in[:], neg_max[:], SINK, None, ALU.add).then_inc(s["sink_in_done"], 1)

                def leaky(c):
                    dve.wait_ge(s[f"e_small{c}"], t.prev)
                    if not t.first1:
                        dve.wait_ge(s[f"p_done{c}"], t.before)
                    dve.scalar_tensor_tensor(out=e[:, c, :], in0=ajm[:, c, :], scalar=z[:, c, AI:AI + 1],
                                             in1=e_small[:, c, :], op0=ALU.add,
                                             op1=ALU.max).then_inc(s[f"e_done{c}"], 1)
                if t.layer1:
                    leaky(0)
                if t.layer0:
                    dve.wait_ge(s["xc_done"], t.now)
                    if not t.first0:
                        dve.wait_ge(s["conv_gates_mm"], t.prev)
                        dve.wait_ge(s["xcl_done"], t.prev)
                    dve.tensor_copy(xch[:], xc[:]).then_inc(s["xch_done"], 1)
                    dve.wait_ge(s["xch_done"], t.now)
                    dve.tensor_tensor(xcl[:], xc[:], xch[:].bitcast(F32), ALU.subtract).then_inc(s["xcl_done"], 1)
                if t.layer1:
                    leaky(1)
                if t.layer1:
                    leaky(2)
                    leaky(3)
                if t.layer0:
                    dve.wait_ge(s["xnh_done"], t.now)
                    if not t.first0:
                        dve.wait_ge(s["gates_mm"], t.prev)
                    dve.tensor_tensor(xnl[:], B_A[:], xnh[:].bitcast(F32), ALU.subtract).then_inc(s["xnl_done"], 1)
                if t.layer1:
                    for c in (1, 3):
                        dve.wait_ge(s[f"pT_mm{c}"], t.prev)
                        if not t.first1:
                            dve.wait_ge(s["att_mm"], t.before)
                        dve.tensor_copy(pT[:, :, c * P:(c + 1) * P],
                                        B_C[:].rearrange("p (m n) -> p m n", m=C)).then_inc(s[f"pT_done{c}"], 1)
                    dve.wait_ge(s["sink_done"], t.prev)
                    dve.wait_ge(s["p_done3"], t.prev)
                    if not t.first1:
                        dve.wait_ge(s["rden_done"], t.before)
                    dve.tensor_tensor(den[:], row_sum[:], sink[:], ALU.add).then_inc(s["den_done"], 1)
                    dve.wait_ge(s["den_done"], t.prev)
                    if not t.first1:
                        dve.wait_ge(s["y2_done"], t.before)
                    dve.reciprocal(rden[:], den[:]).then_inc(s["rden_done"], 1)
                if t.final:
                    dve.wait_ge(s["rstd2_done"], t.before)
                    dve.wait_ge(out_free, t.stored)
                    for c in range(C):
                        last = dve.tensor_scalar(out_sb[:, c, :], y2[:, c, :], mv2[:, c, 0:1], rstd2[:, c:c + 1],
                                                 ALU.subtract, ALU.mult)
                    last.then_inc(s["out_done"], 1)
                if t.layer0:
                    dve.wait_ge(adj_loaded, t.loaded)
                    if t.layer1:
                        dve.wait_ge(s["ajm_done3"], t.prev)
                    dve.tensor_scalar(no_edge[:], adj_in[:], 0.0, MASKED, ALU.is_le,
                                      ALU.mult).then_inc(s["no_edge_done"], 1)

            def layer_norm_stats(when, src, ready, stats, mv, var_eps, tag, eps):
                dve.wait_ge(s[ready], when)
                for c in range(C):
                    last = dve.bn_stats(stats[:, c, :], src[:, c * P:(c + 1) * P])
                last.then_inc(s[f"stats{tag}_done"], 1)
                dve.wait_ge(constants_ready, 1)
                dve.wait_ge(s[f"stats{tag}_done"], when)
                for c in range(C):
                    last = dve.bn_aggr(mv[:, c, :], stats[:, c, :])
                last.then_inc(s[f"mv{tag}_done"], 1)
                dve.wait_ge(s[f"mv{tag}_done"], when)
                dve.tensor_scalar(var_eps[:], mv[:, :, 1], eps, None, ALU.add).then_inc(s[f"var{tag}_done"], 1)

            run_turns(dve, turn)

        @block.tensor
        def _(pe):
            def three(out, w, r, start, stop):
                pe.matmul(out, w[0], r[0], start=start, stop=False)
                pe.matmul(out, w[0], r[1], start=False, stop=False)
                return pe.matmul(out, w[1], r[0], start=False, stop=stop)

            def weight(k):
                return wh[:, k, :], wl[:, k, :]

            conv2_by_tap = raw_conv2[:].rearrange("p (i k) -> p i k", k=TAPS)
            raws = [raw_conv1[:]] + [conv2_by_tap[:, :, k] for k in range(TAPS)] \
                + [raw_ih[:, a, 0:D] for a in range(3)] + [raw_ih[:, a, D:2 * D] for a in range(3)] \
                + [raw_hh[:, a, :] for a in range(3)]
            pe.wait_ge(constants_ready, 1)
            pe.wait_ge(weights_loaded, 7 * 16)
            pe.wait_ge(params_loaded, 18 * 16)
            pe.transpose(B_C[:, 0:D], raw_msg[:], ident[:])
            pe.transpose(B_C[:, D:D + SE], raw_se[:], ident[0:SE, 0:SE])
            pe.transpose(B_C[:, 256:256 + D], raw_W[:], ident[:])
            pe.matmul(B_C[:, 256 + D:256 + D + 2], raw_W[:], att_w[:], start=True, stop=True)
            pe.matmul(B_D[:, 0:2], bW_col[:].to_broadcast([P, P]), att_w[:], start=True,
                      stop=True).then_inc(att_folded, 1)
            for k, raw in enumerate(raws):
                if k % C == 0 and k >= 4 * C:
                    pe.wait_ge(w_split, k // C - 3)
                last = pe.transpose(chunk(bank[(k // C) % 4], k % C), raw, ident[:])
                if k % C == C - 1 or k == len(raws) - 1:
                    last.then_inc(w_turned, 1)
            pe.wait_ge(w_split, -(-NW // C))
            pe.wait_ge(aug_copied, 7)

            X, H, XC, XN = (xh, xl), (hh, hl), (xch, xcl), (xnh, xnl)

            def full(pr):
                return pr[0][:], pr[1][:]

            def turn(t):
                def conv2(first, end):
                    for k in range(first, end):
                        last = three(B_CONV[:], weight(CONV2 + k), (hh[:, k:k + N], hl[:, k:k + N]),
                                     k == 0, k == TAPS - 1)
                    if end == TAPS:
                        last.then_inc(s["conv2_mm"], 1)

                def dist_adj(c):
                    if c == 0:
                        pe.wait_ge(s["U_done"], t.now)
                        pe.wait_ge(s["V_done"], t.now)
                        pe.wait_ge(adj_loaded, t.loaded)
                    else:
                        pe.wait_ge(s[f"E_done{c - 1}"], t.now)
                    pe.matmul(B_A[:], U[:, c * P:(c + 1) * P], V[:], start=True, stop=True).then_inc(s[f"dist_mm{c}"], 1)
                    if c == 0:
                        pe.wait_ge(s["msg_raw1"], t.now)
                    elif c == 1:
                        if t.layer1:
                            pe.wait_ge(s["q2_done"], t.prev)
                    else:
                        pe.wait_ge(s[f"AT_done{c - 2}"], t.now)
                    for n in range(C):
                        last = pe.transpose(chunk((B_B, B_IN)[c % 2], n), adj_in[:, n, c * P:(c + 1) * P], ident[:])
                    last.then_inc(s[f"adjT_mm{c}"], 1)

                def p_turn(c):
                    b = B_D if c % 2 == 0 else B_C
                    pe.wait_ge(s[f"p_done{c}"], t.prev)
                    if c >= 2:
                        pe.wait_ge(s[f"pT_done{c - 2}"], t.prev)
                    for m in range(C):
                        last = pe.transpose(chunk(b, m), p[:, c, m * P:(m + 1) * P], ident[:])
                    last.then_inc(s[f"pT_mm{c}"], 1)

                if t.layer0:
                    pe.wait_ge(x_loaded, t.loaded)
                    if not t.first0:
                        pe.wait_ge(s["xnl_done"], t.prev)
                    for c in range(C):
                        last = pe.transpose(chunk(B_A, c), x_in[:, c, :], ident[:])
                    last.then_inc(s["xT_mm"], 1)
                if t.layer1:
                    pe.wait_ge(s["xnl_done"], t.prev)
                    for a, b in enumerate((B_R, B_Z, B_IN)):
                        last = three(b[:], weight(IH_MSG + a), full(XN), False, True)
                    last.then_inc(s["gates_mm"], 1)
                if t.final:
                    pe.wait_ge(s["oT_done"], t.before)
                    for c in range(C):
                        last = pe.transpose(chunk(B_C, c), oT[:, c * P:(c + 1) * P], ident[:])
                    last.then_inc(s["o_mm"], 1)
                if t.layer0:
                    pe.wait_ge(s["xl_done"], t.now)
                    if not t.first0:
                        pe.wait_ge(s["AT_done3"], t.prev)
                    three(B_B[:], weight(CONV1), full(X), True, True).then_inc(s["conv1_mm"], 1)
                    if t.layer1:
                        pe.wait_ge(s["ghb_done"], t.prev)
                    three(B_HN[:], weight(HH + 2), full(X), True, True).then_inc(s["hn_mm"], 1)
                    for k, b in enumerate((B_A, B_B)):
                        if k == 0:
                            pe.wait_ge(s["xh_done"], t.now)
                        else:
                            pe.wait_ge(s["h1_done"], t.now)
                        for c in (2 * k, 2 * k + 1):
                            last = three(pair(b)[:, c % 2, :], (chunk(xh, c), chunk(xl, c)),
                                         (msg_wh[:], msg_wl[:]), True, True)
                        last.then_inc(s[f"msg_mm{k}"], 1)
                    if t.layer1:
                        pe.wait_ge(s["tz_done"], t.prev)
                    three(B_Z[:], weight(HH + 1), full(X), True, False)
                    pe.wait_ge(s["hl_done"], t.now)
                    conv2(0, 5)
                if t.layer1:
                    pe.wait_ge(s["y_done"], t.prev)
                    if not t.first1:
                        pe.wait_ge(s["y2_done"], t.before)
                    for c in range(C):
                        last = pe.transpose(chunk(B_C, c), y[:, c * P:(c + 1) * P], ident[:])
                    last.then_inc(s["yT_mm"], 1)
                if t.layer0:
                    conv2(5, 6)
                    pe.wait_ge(constants_ready, 7)
                    pe.wait_ge(s["uv_done"], t.now)
                    pe.wait_ge(s["msg_raw0"], t.now)
                    for c in range(C):
                        last = pe.transpose(B_A[0:VOFF + KU, c * P:(c + 1) * P], uv[:, c, :], ident[:])
                    last.then_inc(s["uv_mm"], 1)
                    conv2(6, 8)
                    dist_adj(0)
                    conv2(8, 9)
                    dist_adj(1)
                    conv2(9, 10)
                if t.layer1:
                    pe.wait_ge(s["x1_done"], t.prev)
                    if not t.first1:
                        pe.wait_ge(s["oT_done"], t.before)
                    for c in range(C):
                        last = pe.transpose(chunk(B_D, c), x1[:, c, :], ident[:])
                    last.then_inc(s["x1T_mm"], 1)
                if t.layer0:
                    dist_adj(2)
                    conv2(10, 12)
                if t.layer1:
                    pe.wait_ge(s["x1l_done"], t.prev)
                    for k, b in enumerate((B_C, B_D)):
                        for c in (2 * k, 2 * k + 1):
                            last = three(pair(b)[:, c % 2, :], (chunk(x1h, c), chunk(x1l, c)),
                                         (z_wh[:], z_wl[:]), True, True)
                        last.then_inc(s[f"z_mm{k}"], 1)
                if t.layer0:
                    dist_adj(3)
                    conv2(12, 14)
                if t.layer1:
                    pe.wait_ge(s["z_done1"], t.prev)
                    for c in range(C):
                        last = pe.transpose(chunk(B_C, c), z[:, c, AJ:AJ + 1].to_broadcast([P, P]), ident[:])
                    last.then_inc(s["ajb_mm"], 1)
                if t.layer0:
                    conv2(14, TAPS)
                    pe.wait_ge(s["msg_done"], t.now)
                    pe.wait_ge(s["AT_done3"], t.now)
                    for c in range(C):
                        last = pe.matmul(B_A[:], msg[:, c, :], AT[:, c, :], start=(c == 0), stop=(c == C - 1))
                    last.then_inc(s["nmp_mm"], 1)
                if t.layer0:
                    pe.wait_ge(s["conv_sum_done"], t.now)
                    three(B_R[:], weight(HH), full(X), True, False).then_inc(s["xgates_mm"], 1)
                    pe.wait_ge(s["xcl_done"], t.now)
                    three(B_Z[:], weight(IH_CONV + 1), full(XC), False, False)
                if t.layer1:
                    p_turn(0)
                    p_turn(1)
                if t.layer0:
                    pe.wait_ge(s["AT_done3"], t.now)
                    three(B_IN[:], weight(IH_CONV + 2), full(XC), True, False)
                if t.layer1:
                    p_turn(2)
                    p_turn(3)
                if t.layer0:
                    three(B_R[:], weight(IH_CONV), full(XC), False, False).then_inc(s["conv_gates_mm"], 1)
                if t.layer1:
                    pe.wait_ge(s["pT_done2"], t.prev)
                    pe.wait_ge(s["pT_done3"], t.prev)
                    for c in range(C):
                        last = pe.matmul(B_D[:], z[:, c, 0:D], pT[:, c, :], start=(c == 0), stop=(c == C - 1))
                    last.then_inc(s["att_mm"], 1)

            run_turns(pe, turn)


_IN = ['x', 'adj', 'L0_gnn_w_se', 'L0_gnn_b_se', 'L0_gnn_conv1_w', 'L0_gnn_bn1_g', 'L0_gnn_bn1_b',
       'L0_gnn_bn1_m', 'L0_gnn_bn1_v', 'L0_gnn_conv2_w', 'L0_gnn_bn2_g', 'L0_gnn_bn2_b',
       'L0_gnn_bn2_m', 'L0_gnn_bn2_v', 'L0_gnn_w_msg', 'L0_gnn_b_msg', 'L0_gnn_w_ih', 'L0_gnn_b_ih',
       'L0_gnn_w_hh', 'L0_gnn_b_hh', 'L1_gnn_W', 'L1_gnn_bW', 'L1_gnn_wai', 'L1_gnn_bai',
       'L1_gnn_waj', 'L1_gnn_baj']


def kernel(**inputs):
    import numpy as _np
    import concourse.bacc as _bacc
    from concourse import mybir as _mybir
    from concourse.bass_utils import run_bass_kernel_spmd as _run

    nc = _bacc.Bacc("TRN2", target_bir_lowering=False, num_devices=1)
    arrays, args = {}, []
    for name in _IN:
        a = _np.ascontiguousarray(inputs[name])
        arrays[f"in_{name}_dram"] = a
        args.append(nc.dram_tensor(f"in_{name}_dram", a.shape, _mybir.dt.from_np(a.dtype),
                                   kind="ExternalInput").ap())
    out = nc.dram_tensor("out_dram", inputs["x"].shape, _mybir.dt.float32, kind="ExternalOutput").ap()
    resnorm_kernel(nc, *args, out)
    r = _run(nc, [arrays], core_ids=[0])
    return r.results[0]["out_dram"]
```

```python
import concourse.bass as bass
from concourse import mybir
from contextlib import ExitStack

F32 = mybir.dt.float32
F32R = mybir.dt.float32r
ALU = mybir.AluOpType
ACT = mybir.ActivationFunctionType


class Turn:

    def __init__(self, parity, before, prev, now, loaded, stored, layer0=True, layer1=True,
                 final=True, first0=False, first1=False):
        self.parity = parity
        self.now = now
        self.prev = prev
        self.before = before
        self.loaded = loaded
        self.stored = stored
        self.layer0, self.layer1, self.final = layer0, layer1, final
        self.first0 = first0
        self.first1 = first1


def resnorm_kernel(nc, x, adj, w_se, b_se, conv1_w, bn1_g, bn1_b, bn1_m, bn1_v, conv2_w, bn2_g,
                   bn2_b, bn2_m, bn2_v, w_msg, b_msg, w_ih, b_ih, w_hh, b_hh, W, bW, wai, bai,
                   waj, baj, out):
    G, N, D = x.shape
    P = 128
    C = N // P
    TAPS = conv2_w.shape[2]
    PAD = TAPS // 2
    SE = w_se.shape[0]
    AUG = D + 4
    KU = 4 * SE + 4
    VOFF = 32
    EPS = 1e-5
    ALPHA = 0.2
    SINK = -1e9
    MASKED = -9e15 / ALPHA

    ctx = ExitStack()
    with ctx:
        def sb(name, shape, dt=F32):
            return ctx.enter_context(nc.sbuf_tensor(name, shape, dt))

        def sem(name):
            return ctx.enter_context(nc.semaphore(name))

        ctx.enter_context(nc.allow_non_contiguous_dma("parameter vectors as columns, once"))

        ident = sb("ident", [P, P])
        half_power = sb("half_power", [P, C])
        raw_conv1 = sb("raw_conv1", [P, D])
        raw_conv2 = sb("raw_conv2", [P, D * TAPS])
        EVEN, ODD = TAPS // 2 + 1, TAPS // 2
        raw_sums = sb("raw_sums", [P, ODD, D])
        raw_msg = sb("raw_msg", [P, D])
        raw_se = sb("raw_se", [SE, D])
        raw_ih = sb("raw_ih", [P, 3, 2 * D])
        raw_hh = sb("raw_hh", [P, 3, D])
        raw_W = sb("raw_W", [P, D])
        NW = 1 + ODD + TAPS + 9
        wh = sb("wh", [P, NW, D], F32R)
        wl = sb("wl", [P, NW, D], F32R)
        CONV1, CONV_SUM, CONV2 = 0, 1, 1 + ODD
        IH_CONV, IH_MSG, HH = CONV2 + TAPS, CONV2 + TAPS + 3, CONV2 + TAPS + 6
        msg_wh = sb("msg_wh", [P, AUG], F32R)
        msg_wl = sb("msg_wl", [P, AUG], F32R)
        z_wh = sb("z_wh", [P, AUG], F32R)
        z_wl = sb("z_wl", [P, AUG], F32R)
        aug_full = sb("aug_full", [P, 2, AUG])
        bn = sb("bn", [P, 8])
        bn_scale = sb("bn_scale", [P, 2])
        bn_shift = sb("bn_shift", [P, 2])
        bn_tmp = sb("bn_tmp", [P, 2])
        gru_bi = sb("gru_bi", [P, 3])
        gru_bh = sb("gru_bh", [P, 3])
        gru_half = sb("gru_half", [P, 3])
        msg_bias = sb("msg_bias", [P, AUG])
        z_bias = sb("z_bias", [P, AUG])
        att_w = sb("att_w", [P, 2])
        bW_col = sb("bW_col", [P, 1])
        att_b = sb("att_b", [P, 2])

        x_in = sb("x_in", [P, C, D])
        adj_in = sb("adj_in", [P, C, N])
        xT = sb("xT", [P, 2, N])
        xh, xl = sb("xh", [P, N], F32R), sb("xl", [P, N], F32R)
        HALF = N // 2
        HW = HALF + PAD
        h1 = sb("h1", [P, N + 4])
        h_diff = sb("h_diff", [P, 2, HW])
        hh, hl = sb("hh", [P, 3, HW], F32R), sb("hl", [P, 3, HW], F32R)
        x_shared = sb("x_shared", [P, N])
        msg_raw = sb("msg_raw", [P, C, AUG])
        msg = sb("msg", [P, C, D])
        s_sq = sb("s_sq", [P, C, SE])
        sq_a, sq_b = sb("sq_a", [P, C, 1]), sb("sq_b", [P, C, 1])
        uv = sb("uv", [P, C, VOFF + KU])
        U, V = sb("U", [KU, N], F32R), sb("V", [KU, N], F32R)
        E = sb("E", [P, 2, N])
        AT = sb("AT", [P, C, N])
        conv_sum = sb("conv_sum", [P, N])
        xc = sb("xc", [P, N])
        xch, xcl = sb("xch", [P, N], F32R), sb("xcl", [P, N], F32R)
        xnh, xnl = sb("xnh", [P, N], F32R), sb("xnl", [P, N], F32R)
        tr, tz, ghb = sb("tr", [P, N]), sb("tz", [P, N]), sb("ghb", [P, N])
        q1, q2, nn = sb("q1", [P, N]), sb("q2", [P, N]), sb("nn", [P, N])
        x_part, n_part, y = sb("x_part", [P, N]), sb("n_part", [P, N]), sb("y", [P, N])
        stats = sb("stats", [P, C, 6])
        mv = sb("mv", [P, C, 2])
        var_eps, rstd = sb("var_eps", [P, C]), sb("rstd", [P, C])
        x1 = sb("x1", [P, 2, C, D])
        x1h, x1l = sb("x1h", [P, N], F32R), sb("x1l", [P, N], F32R)
        z = sb("z", [P, C, AUG])
        AJ, AI = D, D + 1
        no_edge = sb("no_edge", [P, C, N])
        ajm = sb("ajm", [P, C, N])
        amax, u_max, leaky_max = sb("amax", [P, C]), sb("u_max", [P, C]), sb("leaky_max", [P, C])
        neg_max, sink_in, sink = sb("neg_max", [P, C]), sb("sink_in", [P, C]), sb("sink", [P, C])
        ai_small = sb("ai_small", [P, C])
        e_small = sb("e_small", [P, C, N])
        e = sb("e", [P, C, N])
        p = sb("p", [P, C, N])
        row_sum, den, rden = sb("row_sum", [P, C]), sb("den", [P, C]), sb("rden", [P, C])
        pT = sb("pT", [P, C, N])
        oT = sb("oT", [P, N])
        y2 = sb("y2", [P, C, D])
        stats2, mv2 = sb("stats2", [P, C, 6]), sb("mv2", [P, C, 2])
        var_eps2, rstd2 = sb("var_eps2", [P, C]), sb("rstd2", [P, C])
        out_sb = sb("out_sb", [P, C, D])

        bank = [ctx.enter_context(nc.psum_tensor(f"bank{k}", [P, N], F32)) for k in range(8)]
        B_CONV = B_R = bank[0]
        B_Z, B_IN, B_HN = bank[1], bank[2], bank[3]
        B_A, B_B = bank[4], bank[5]
        B_C, B_D = bank[6], bank[7]

        def chunk(ap, c, width=P):
            return ap[:, c * width:(c + 1) * width]

        def pair(b):
            return b[:, 0:2 * AUG].rearrange("p (c f) -> p c f", c=2)

        params_loaded, weights_loaded = sem("params_loaded"), sem("weights_loaded")
        ident_zero, constants_ready = sem("ident_zero"), sem("constants_ready")
        w_turned, w_split, w_high = sem("w_turned"), sem("w_split"), sem("w_high")
        att_folded, aug_copied = sem("att_folded"), sem("aug_copied")
        setup_dve, setup_pow = sem("setup_dve"), sem("setup_pow")
        params_ready, taps_summed, borders_ready = sem("params_ready"), sem("taps_summed"), sem("borders_ready")
        x_loaded, adj_loaded, out_free = sem("x_loaded"), sem("adj_loaded"), sem("out_free")
        s = {n: sem(n) for n in (
            "xT_mm xT_done xh_done xl_done conv1_mm h1_done h_diff_done hho_done hlo_done hhd_done hld_done "
            "msg_mm0 msg_mm1 msg_raw0 msg_raw1 msg_done "
            "uv_sh uv_sl uv_squares uv_sum1 uv_sum uv_sqh uv_sql uv_done uv_mm U_done V_done "
            "dist_mm0 dist_mm1 dist_mm2 dist_mm3 adjT_mm0 adjT_mm1 adjT_mm2 adjT_mm3 "
            "E_done0 E_done1 E_done2 E_done3 AT_done0 AT_done1 AT_done2 AT_done3 "
            "no_edge_done shared_mm x_shared_done conv2_mm conv_sum_done xc_done xch_done xcl_done nmp_mm xnh_done xnl_done "
            "hn_mm xgates_mm conv_gates_mm gates_mm ghb_done tr_done tz_done q1_done q2_done "
            "nn_done x_part_done n_part_done y_done "
            "yT_mm stats_done mv_done var_done rstd_done x1_done x1T_mm x1h_done x1l_done "
            "z_mm0 z_mm1 z_done0 z_done1 ajb_mm ai_small_done "
            "ajm_done0 ajm_done1 ajm_done2 ajm_done3 u_max_done leaky_max_done neg_max_done "
            "sink_in_done sink_done e_small0 e_small1 e_small2 e_small3 e_done0 e_done1 e_done2 "
            "e_done3 p_done0 p_done1 p_done2 p_done3 pT_mm0 pT_mm1 pT_mm2 pT_mm3 "
            "pT_done0 pT_done1 pT_done2 pT_done3 att_mm oT_done o_mm den_done rden_done "
            "y2_done stats2_done mv2_done var2_done rstd2_done out_done").split()}

        x_dram = x.rearrange("g (c p) d -> g p c d", p=P)
        adj_dram = adj.rearrange("g (c p) m -> g p c m", p=P)
        out_dram = out.rearrange("g (c p) d -> g p c d", p=P)

        def column(v):
            return v.rearrange("(p a) -> p a", a=1)

        def row_everywhere(v):
            return v.rearrange("(a n) -> a n", a=1).to_broadcast([P, v.shape[0]])

        def run_turns(eng, turn):
            turn(Turn(0, None, None, 1, 16, None, layer1=False, final=False, first0=True))
            turn(Turn(1, None, 1, 2, 32, None, final=False, first1=True))
            regs = {}
            for name in ("gm1", "g0", "g1", "g2", "s0", "s1", "s2", "s3"):
                regs[name] = eng.alloc_register(name)
            with eng.Fori(2, G, 2) as g:
                for k, name in enumerate(("gm1", "g0", "g1", "g2")):
                    eng.reg_add(regs[name], g, k - 1)
                for k in range(4):
                    eng.reg_mul(regs[f"s{k}"], regs[("gm1", "g0", "g1", "g2")[k]], 16)
                v = {name: eng.snap(r, min_val=1) for name, r in regs.items()}
                turn(Turn(0, v["gm1"], v["g0"], v["g1"], v["s2"], v["s0"]))
                turn(Turn(1, v["g0"], v["g1"], v["g2"], v["s3"], v["s1"]))
            turn(Turn(G % 2, G - 1, G, None, None, 16 * (G - 1), layer0=False))
            turn(Turn((G + 1) % 2, G, None, None, None, 16 * G, layer0=False, layer1=False))

        block = ctx.enter_context(nc.Block())

        @block.sync
        def _(sp):
            sp.dma_start(x_in[:], x_dram[0]).then_inc(x_loaded, 16)
            sp.dma_start(raw_conv1[:], conv1_w.rearrange("o i k -> o (i k)")).then_inc(weights_loaded, 16)
            sp.dma_start(raw_conv2[:], conv2_w.rearrange("o i k -> o (i k)")).then_inc(weights_loaded, 16)
            sp.dma_start(raw_msg[:], w_msg).then_inc(weights_loaded, 16)
            sp.dma_start(raw_se[:], w_se).then_inc(weights_loaded, 16)
            sp.dma_start(raw_ih[:], w_ih.rearrange("(a o) i -> o a i", a=3)).then_inc(weights_loaded, 16)
            sp.dma_start(raw_hh[:], w_hh.rearrange("(a o) i -> o a i", a=3)).then_inc(weights_loaded, 16)
            sp.dma_start(raw_W[:], W).then_inc(weights_loaded, 16)
            sp.dma_start(adj_in[:], adj_dram[0]).then_inc(adj_loaded, 16)

            def load_x(g, here):
                sp.wait_ge(s["xT_mm"], here)
                sp.dma_start(x_in[:], x_dram[g]).then_inc(x_loaded, 16)

            def load_adj(g, here):
                sp.wait_ge(s["adjT_mm3"], here)
                sp.wait_ge(s["no_edge_done"], here)
                sp.dma_start(adj_in[:], adj_dram[g]).then_inc(adj_loaded, 16)

            def store(g, here):
                sp.wait_ge(s["out_done"], here)
                sp.dma_start(out_dram[g], out_sb[:]).then_inc(out_free, 16)

            for g in range(2):
                load_x(g + 1, g + 1)
                load_adj(g + 1, g + 1)
            with sp.Fori(2, G - 1) as g:
                load_x(g + 1, g + 1)
                load_adj(g + 1, g + 1)
                store(g - 2, g - 1)
            store(G - 3, G - 2)
            store(G - 2, G - 1)
            store(G - 1, G)
            sp.wait_ge(out_free, 16 * (G + 1))

        @block.gpsimd
        def _(pool):
            pool.memset(ident[:], 0.0).then_inc(ident_zero, 1)
            pool.wait_ge(ident_zero, 1)
            pool.affine_select(out=ident[:], in_=ident[:], compare_op=ALU.not_equal, fill=1.0, base=0,
                               pattern=[[-1, P]], channel_multiplier=1).then_inc(constants_ready, 1)
            pool.memset(half_power[:], -0.5).then_inc(constants_ready, 1)
            pool.memset(hh[:].bitcast(F32), 0.0).then_inc(constants_ready, 1)
            pool.memset(hl[:].bitcast(F32), 0.0).then_inc(constants_ready, 1)
            pool.memset(uv[:], 0.0).then_inc(constants_ready, 1)
            pool.memset(h1[:], 0.0)
            pool.memset(h_diff[:], 0.0).then_inc(borders_ready, 1)
            pool.wait_ge(constants_ready, 5)
            pool.memset(uv[:, :, 4 * SE + 2:KU], 1.0).then_inc(constants_ready, 1)
            pool.memset(uv[:, :, VOFF + 4 * SE:VOFF + 4 * SE + 2], -1.0).then_inc(constants_ready, 1)
            pool.wait_ge(weights_loaded, 7 * 16)
            taps = raw_conv2[:].rearrange("p (i k) -> p k i", k=TAPS)
            pool.tensor_tensor(raw_sums[:], taps[:, 0:2 * ODD:2, :], taps[:, 1:2 * ODD:2, :],
                               ALU.add).then_inc(taps_summed, 1)
            pool.wait_ge(setup_dve, 1)
            pool.tensor_tensor(bn_scale[:], bn_tmp[:], half_power[:, 0:2], ALU.pow).then_inc(setup_pow, 1)

            def turn(t):
                if t.layer0:
                    pool.wait_ge(s["h1_done"], t.now)
                    if t.first0:
                        pool.wait_ge(borders_ready, 1)
                    else:
                        pool.wait_ge(s["hhd_done"], t.prev)
                        pool.wait_ge(s["hld_done"], t.prev)
                    pool.tensor_tensor(h_diff[:, 0, PAD // 2:PAD // 2 + HALF], h1[:, 2:2 + N:2],
                                       h1[:, 3:3 + N:2], ALU.subtract)
                    pool.tensor_tensor(h_diff[:, 1, PAD // 2 - 1:PAD // 2 + HALF], h1[:, 2:4 + N:2],
                                       h1[:, 1:3 + N:2], ALU.subtract).then_inc(s["h_diff_done"], 1)
                    def u_view(a):
                        return uv[:, :, 2 * SE * a:2 * SE * (a + 1)].rearrange("p c (b k) -> p c b k", b=2)

                    def v_view(a):
                        return uv[:, :, VOFF:VOFF + 4 * SE].rearrange("p c (b a k) -> p c b a k", b=2, a=2)[:, :, :, a, :]

                    sv = msg_raw[:, :, D:D + SE]

                    def twice(ap):
                        return ap.rearrange("p c (b k) -> p c b k", b=1).to_broadcast([P, C, 2, SE])

                    uq = uv[:, :, 4 * SE:4 * SE + 1]
                    pool.wait_ge(constants_ready, 7)
                    pool.wait_ge(s["msg_raw1"], t.now)
                    pool.wait_ge(s["msg_raw0"], t.now)
                    if not t.first0:
                        pool.wait_ge(s["uv_mm"], t.prev)
                    pool.tensor_copy(u_view(0).bitcast(F32R), twice(sv)).then_inc(s["uv_sh"], 1)
                    pool.tensor_tensor(s_sq[:], sv, sv, ALU.mult).then_inc(s["uv_squares"], 1)
                    pool.wait_ge(s["uv_sh"], t.now)
                    pool.tensor_tensor(u_view(1).bitcast(F32R), twice(sv), u_view(0),
                                       ALU.subtract).then_inc(s["uv_sl"], 1)
                    pool.wait_ge(s["uv_squares"], t.now)
                    pool.tensor_tensor(sq_a[:], s_sq[:, :, 0:1], s_sq[:, :, 1:2],
                                       ALU.add).then_inc(s["uv_sum1"], 1)
                    pool.wait_ge(constants_ready, 7)
                    pool.wait_ge(s["uv_sl"], t.now)
                    pool.tensor_scalar(v_view(0), u_view(0), 2.0, None, ALU.mult)
                    pool.tensor_scalar(v_view(1), u_view(1), 2.0, None, ALU.mult)
                    pool.wait_ge(s["uv_sum1"], t.now)
                    pool.tensor_tensor(sq_b[:], sq_a[:], s_sq[:, :, 2:3], ALU.add).then_inc(s["uv_sum"], 1)
                    pool.wait_ge(constants_ready, 7)
                    pool.wait_ge(s["uv_sum"], t.now)
                    pool.tensor_copy(uq.bitcast(F32R), sq_b[:]).then_inc(s["uv_sqh"], 1)
                    pool.wait_ge(s["uv_sqh"], t.now)
                    pool.tensor_tensor(uv[:, :, 4 * SE + 1:4 * SE + 2].bitcast(F32R), sq_b[:], uq,
                                       ALU.subtract).then_inc(s["uv_sql"], 1)
                    pool.wait_ge(constants_ready, 7)
                    pool.wait_ge(s["uv_sql"], t.now)
                    pool.tensor_scalar(uv[:, :, VOFF + 4 * SE + 2:VOFF + KU],
                                       uv[:, :, 4 * SE:4 * SE + 2], -1.0, None,
                                       ALU.mult).then_inc(s["uv_done"], 1)
                if t.layer1:
                    pool.wait_ge(s["var_done"], t.prev)
                    pool.tensor_tensor(rstd[:], var_eps[:], half_power[:], ALU.pow).then_inc(s["rstd_done"], 1)
                if t.final:
                    pool.wait_ge(s["var2_done"], t.before)
                    pool.tensor_tensor(rstd2[:], var_eps2[:], half_power[:], ALU.pow).then_inc(s["rstd2_done"], 1)

            run_turns(pool, turn)

        @block.scalar
        def _(act):
            for k, v in enumerate((bn1_g, bn1_b, bn1_m, bn1_v, bn2_g, bn2_b, bn2_m, bn2_v)):
                act.dma_start(bn[:, k:k + 1], column(v)).then_inc(params_loaded, 16)
            act.dma_start(gru_bi[:], b_ih.rearrange("(a p) -> p a", a=3)).then_inc(params_loaded, 16)
            act.dma_start(gru_bh[:], b_hh.rearrange("(a p) -> p a", a=3)).then_inc(params_loaded, 16)
            act.dma_start(msg_bias[:, 0:D], row_everywhere(b_msg)).then_inc(params_loaded, 16)
            act.dma_start(msg_bias[:, D:D + SE], row_everywhere(b_se)).then_inc(params_loaded, 16)
            act.dma_start(z_bias[:, 0:D], row_everywhere(bW)).then_inc(params_loaded, 16)
            act.dma_start(att_w[:, 0:1], waj.rearrange("a p -> p a")).then_inc(params_loaded, 16)
            act.dma_start(att_w[:, 1:2], wai.rearrange("a p -> p a")).then_inc(params_loaded, 16)
            act.dma_start(bW_col[:], column(bW)).then_inc(params_loaded, 16)
            act.dma_start(att_b[:, 0:1], row_everywhere(baj)).then_inc(params_loaded, 16)
            act.dma_start(att_b[:, 1:2], row_everywhere(bai)).then_inc(params_loaded, 16)

            def turn(t):
                par = t.parity

                def exp_dist(c):
                    act.wait_ge(s[f"dist_mm{c}"], t.now)
                    if c >= 2:
                        act.wait_ge(s[f"AT_done{c - 2}"], t.now)
                    elif not t.first0:
                        act.wait_ge(s[f"AT_done{c + 2}"], t.prev)
                    act.activation(E[:, c % 2, :], B_A[:], ACT.Exp).then_inc(s[f"E_done{c}"], 1)

                def p_out(c):
                    act.wait_ge(s[f"pT_mm{c}"], t.before)
                    act.activation(pT[:, :, c * P:(c + 1) * P], B_D[:].rearrange("p (m n) -> p m n", m=C),
                                   ACT.Copy).then_inc(s[f"pT_done{c}"], 1)

                if t.layer1:
                    act.wait_ge(s["hn_mm"], t.prev)
                    act.wait_ge(params_ready, 1)
                    if not t.first1:
                        act.wait_ge(s["q1_done"], t.before)
                    act.activation(ghb[:], B_HN[:], ACT.Identity, bias=gru_half[:, 2:3],
                                   scale=0.5).then_inc(s["ghb_done"], 1)
                if t.layer0:
                    act.wait_ge(s["xT_mm"], t.now)
                    if t.layer1 and not t.first1:
                        act.wait_ge(s["x_part_done"], t.before)
                    act.activation(xT[:, par, :], B_A[:], ACT.Copy).then_inc(s["xT_done"], 1)
                    if not t.first0:
                        act.wait_ge(s["xgates_mm"], t.prev)
                        act.wait_ge(s["xl_done"], t.prev)
                    act.activation(xh[:], B_A[:], ACT.Copy).then_inc(s["xh_done"], 1)
                if t.layer1:
                    act.wait_ge(s["gates_mm"], t.prev)
                    if not t.first1:
                        act.wait_ge(s["q1_done"], t.before)
                    act.activation(tr[:], B_R[:], ACT.Tanh, bias=gru_half[:, 0:1], scale=0.5).then_inc(s["tr_done"], 1)
                    if not t.first1:
                        act.wait_ge(s["n_part_done"], t.before)
                    act.activation(tz[:], B_Z[:], ACT.Tanh, bias=gru_half[:, 1:2], scale=0.5).then_inc(s["tz_done"], 1)
                if t.final:
                    p_out(0)
                if t.layer0:
                    act.wait_ge(s["conv1_mm"], t.now)
                    act.wait_ge(params_ready, 1)
                    if t.first0:
                        act.wait_ge(borders_ready, 1)
                    else:
                        act.wait_ge(s["hlo_done"], t.prev)
                        act.wait_ge(s["h_diff_done"], t.prev)
                    act.activation(h1[:, 2:2 + N], B_B[:], ACT.Relu, bias=bn_shift[:, 0:1],
                                   scale=bn_scale[:, 0:1]).then_inc(s["h1_done"], 1)
                    act.wait_ge(s["h1_done"], t.now)
                    if t.first0:
                        act.wait_ge(constants_ready, 4)
                    else:
                        act.wait_ge(s["conv2_mm"], t.prev)
                    act.activation(hh[:, 0, PAD // 2:PAD // 2 + HALF], h1[:, 3:3 + N:2],
                                   ACT.Copy).then_inc(s["hho_done"], 1)
                if t.final:
                    p_out(2)
                if t.layer1:
                    act.wait_ge(s["q2_done"], t.prev)
                    if not t.first1:
                        act.wait_ge(s["n_part_done"], t.before)
                    act.activation(nn[:], q2[:], ACT.Tanh, bias=gru_bi[:, 2:3]).then_inc(s["nn_done"], 1)
                if t.layer0:
                    act.wait_ge(s["h_diff_done"], t.now)
                    if not t.first0:
                        act.wait_ge(s["conv2_mm"], t.prev)
                        act.wait_ge(s["hld_done"], t.prev)
                    act.activation(hh[:, 1:3, :], h_diff[:], ACT.Copy).then_inc(s["hhd_done"], 1)
                if t.layer0:
                    act.wait_ge(s["msg_raw1"], t.now)
                    if not t.first0:
                        act.wait_ge(s["nmp_mm"], t.prev)
                    act.activation(msg[:], msg_raw[:, :, 0:D], ACT.Relu).then_inc(s["msg_done"], 1)
                if t.final:
                    act.wait_ge(s["att_mm"], t.before)
                    act.activation(oT[:], B_D[:], ACT.Copy).then_inc(s["oT_done"], 1)
                if t.layer0:
                    act.wait_ge(s["uv_mm"], t.now)
                    if not t.first0:
                        act.wait_ge(s["dist_mm3"], t.prev)
                    act.activation(V[:], B_A[VOFF:VOFF + KU, :], ACT.Copy).then_inc(s["V_done"], 1)
                if t.layer1:
                    act.wait_ge(s["x1T_mm"], t.prev)
                    if not t.first1:
                        act.wait_ge(s["z_mm1"], t.before)
                    act.activation(x1h[:], B_C[:], ACT.Copy).then_inc(s["x1h_done"], 1)
                if t.layer0:
                    exp_dist(0)
                    exp_dist(1)
                    exp_dist(2)
                    exp_dist(3)
                if t.layer1:
                    for c in range(C):
                        act.wait_ge(s[f"ajm_done{c}"], t.prev)
                        if c == 0:
                            act.wait_ge(s["ai_small_done"], t.prev)
                        if not t.first1:
                            act.wait_ge(s[f"e_done{c}"], t.before)
                        act.activation(e_small[:, c, :], ajm[:, c, :], ACT.Identity, bias=ai_small[:, c:c + 1],
                                       scale=ALPHA).then_inc(s[f"e_small{c}"], 1)
                if t.layer0:
                    act.wait_ge(s["conv_sum_done"], t.now)
                    if not t.first0:
                        act.wait_ge(s["xcl_done"], t.prev)
                    act.activation(xc[:], conv_sum[:], ACT.Relu, bias=bn_shift[:, 1:2]).then_inc(s["xc_done"], 1)
                if t.layer1:
                    act.wait_ge(s["sink_in_done"], t.prev)
                    if not t.first1:
                        act.wait_ge(s["den_done"], t.before)
                    act.activation(sink[:], sink_in[:], ACT.Exp).then_inc(s["sink_done"], 1)
                    for c in range(C):
                        act.wait_ge(s[f"e_done{c}"], t.prev)
                        if not t.first1:
                            act.wait_ge(s[f"pT_mm{c}"], t.before)
                            if c == 0:
                                act.wait_ge(s["den_done"], t.before)
                        act.activation(p[:, c, :], e[:, c, :], ACT.Exp, bias=neg_max[:, c:c + 1],
                                       accum_out=row_sum[:, c:c + 1]).then_inc(s[f"p_done{c}"], 1)
                        if t.layer0 and c == 1:
                            act.wait_ge(s["nmp_mm"], t.now)
                            if not t.first0:
                                act.wait_ge(s["gates_mm"], t.prev)
                            act.activation(xnh[:], B_A[:], ACT.Copy).then_inc(s["xnh_done"], 1)
                elif t.layer0:
                    act.wait_ge(s["nmp_mm"], t.now)
                    act.activation(xnh[:], B_A[:], ACT.Copy).then_inc(s["xnh_done"], 1)

            act.wait_ge(params_loaded, 18 * 16)
            run_turns(act, turn)

        @block.vector
        def _(dve):
            bn4 = bn[:].rearrange("p (n k) -> p n k", n=2)
            dve.wait_ge(params_loaded, 18 * 16)
            dve.tensor_scalar(bn_tmp[:], bn4[:, :, 3], EPS, None, ALU.add).then_inc(setup_dve, 1)
            dve.memset(msg_bias[:, D + SE:AUG], 0.0).then_inc(out_free, 16)
            dve.memset(z_bias[:, D + 2:AUG], 0.0)
            dve.memset(aug_full[:], 0.0).then_inc(setup_dve, 1)
            dve.tensor_tensor(gru_half[:, 0:2], gru_bi[:, 0:2], gru_bh[:, 0:2], ALU.add)
            dve.tensor_copy(gru_half[:, 2:3], gru_bh[:, 2:3]).then_inc(setup_dve, 1)
            dve.wait_ge(setup_dve, 3)
            dve.tensor_scalar(gru_half[:], gru_half[:], 0.5, None, ALU.mult).then_inc(setup_dve, 1)
            dve.wait_ge(setup_pow, 1)
            dve.tensor_tensor(bn_scale[:], bn_scale[:], bn4[:, :, 0], ALU.mult).then_inc(setup_dve, 1)
            dve.wait_ge(setup_dve, 5)
            dve.tensor_tensor(bn_tmp[:], bn_scale[:], bn4[:, :, 2], ALU.mult).then_inc(setup_dve, 1)
            dve.wait_ge(setup_dve, 6)
            dve.tensor_tensor(bn_shift[:], bn4[:, :, 1], bn_tmp[:], ALU.subtract).then_inc(params_ready, 1)

            blocks = NW
            for k in range(0, blocks, C):
                n = min(C, blocks - k)
                b = bank[(k // C) % 4]
                src = b[:, 0:n * P].rearrange("p (w o) -> p w o", w=n)
                dve.wait_ge(w_turned, k // C + 1)
                dve.tensor_copy(wh[:, k:k + n, :], src).then_inc(w_high, 1)
                dve.wait_ge(w_high, k // C + 1)
                dve.tensor_tensor(wl[:, k:k + n, :], src, wh[:, k:k + n, :].bitcast(F32),
                                  ALU.subtract).then_inc(w_split, 1)
            groups = -(-blocks // C)
            dve.wait_ge(att_folded, 1)
            dve.wait_ge(setup_dve, 2)
            dve.tensor_copy(aug_full[:, 0, 0:D + SE], B_C[:, 0:D + SE]).then_inc(aug_copied, 1)
            dve.tensor_copy(aug_full[:, 1, 0:D + 2], B_C[:, 256:256 + D + 2]).then_inc(aug_copied, 1)
            dve.tensor_tensor(z_bias[:, D:D + 2], B_D[:, 0:2], att_b[:], ALU.add).then_inc(aug_copied, 1)
            dve.wait_ge(aug_copied, 3)
            dve.tensor_copy(msg_wh[:], aug_full[:, 0, :]).then_inc(aug_copied, 1)
            dve.tensor_copy(z_wh[:], aug_full[:, 1, :]).then_inc(aug_copied, 1)
            dve.wait_ge(aug_copied, 5)
            dve.tensor_tensor(msg_wl[:], aug_full[:, 0, :], msg_wh[:].bitcast(F32),
                              ALU.subtract).then_inc(aug_copied, 1)
            dve.tensor_tensor(z_wl[:], aug_full[:, 1, :], z_wh[:].bitcast(F32),
                              ALU.subtract).then_inc(aug_copied, 1)

            def by_parity(ap):
                return ap.rearrange("p (i e) -> p e i", e=2)

            def bias_pair(b):
                return b[:].rearrange("p (c f) -> p c f", c=1).to_broadcast([P, 2, AUG])

            def turn(t):
                par = t.parity

                def mask_AT(c):
                    dve.wait_ge(s[f"E_done{c}"], t.now)
                    dve.wait_ge(s[f"adjT_mm{c}"], t.now)
                    if not t.first0:
                        dve.wait_ge(s["nmp_mm"], t.prev)
                    dve.tensor_tensor(AT[:, c, :], E[:, c % 2, :], (B_B, B_IN)[c % 2][:],
                                      ALU.mult).then_inc(s[f"AT_done{c}"], 1)

                def p_out(c):
                    dve.wait_ge(s[f"pT_mm{c}"], t.before)
                    dve.tensor_copy(pT[:, :, c * P:(c + 1) * P],
                                    B_C[:].rearrange("p (m n) -> p m n", m=C)).then_inc(s[f"pT_done{c}"], 1)

                if t.layer0:
                    dve.wait_ge(s["xh_done"], t.now)
                    dve.wait_ge(s["xT_done"], t.now)
                    if not t.first0:
                        dve.wait_ge(s["xgates_mm"], t.prev)
                    dve.tensor_tensor(xl[:], xT[:, par, :], xh[:].bitcast(F32),
                                      ALU.subtract).then_inc(s["xl_done"], 1)
                if t.final:
                    if not t.layer1:
                        dve.wait_ge(s["out_done"], G - 1)
                    else:
                        dve.wait_ge(s["no_edge_done"], t.prev)
                    dve.wait_ge(s["sink_done"], t.before)
                    dve.wait_ge(s["p_done3"], t.before)
                    dve.tensor_tensor(den[:], row_sum[:], sink[:], ALU.add).then_inc(s["den_done"], 1)
                    dve.wait_ge(s["den_done"], t.before)
                    dve.reciprocal(rden[:], den[:]).then_inc(s["rden_done"], 1)
                if t.layer1:
                    dve.wait_ge(s["tr_done"], t.prev)
                    dve.wait_ge(s["ghb_done"], t.prev)
                    if not t.first1:
                        dve.wait_ge(s["q2_done"], t.before)
                    dve.scalar_tensor_tensor(out=q1[:], in0=tr[:], scalar=1.0, in1=ghb[:], op0=ALU.add,
                                             op1=ALU.mult).then_inc(s["q1_done"], 1)
                if t.layer1:
                    dve.wait_ge(s["q1_done"], t.prev)
                    if not t.first1:
                        dve.wait_ge(s["nn_done"], t.before)
                    dve.tensor_tensor(q2[:], q1[:], B_IN[:], ALU.add).then_inc(s["q2_done"], 1)
                if t.final:
                    p_out(1)
                if t.layer1:
                    dve.wait_ge(s["tz_done"], t.prev)
                    if not t.first1:
                        dve.wait_ge(s["y_done"], t.before)
                    dve.scalar_tensor_tensor(out=x_part[:], in0=tz[:], scalar=3.0, in1=xT[:, 1 - par, :], op0=ALU.add,
                                             op1=ALU.mult).then_inc(s["x_part_done"], 1)
                if t.layer0:
                    body = slice(PAD // 2, PAD // 2 + HALF)
                    dve.wait_ge(s["hho_done"], t.now)
                    if not t.first0:
                        dve.wait_ge(s["conv2_mm"], t.prev)
                    dve.tensor_tensor(hl[:, 0, body], h1[:, 3:3 + N:2], hh[:, 0, body].bitcast(F32),
                                      ALU.subtract).then_inc(s["hlo_done"], 1)
                if t.final:
                    p_out(3)
                if t.layer1:
                    dve.wait_ge(s["nn_done"], t.prev)
                    dve.wait_ge(s["tz_done"], t.prev)
                    if not t.first1:
                        dve.wait_ge(s["y_done"], t.before)
                    dve.scalar_tensor_tensor(out=n_part[:], in0=tz[:], scalar=-1.0, in1=nn[:], op0=ALU.add,
                                             op1=ALU.mult).then_inc(s["n_part_done"], 1)
                    dve.wait_ge(s["n_part_done"], t.prev)
                    dve.wait_ge(s["x_part_done"], t.prev)
                    if not t.first1:
                        dve.wait_ge(s["yT_mm"], t.before)
                    dve.tensor_tensor(y[:], x_part[:], n_part[:], ALU.subtract).then_inc(s["y_done"], 1)
                if t.layer0:
                    for k, b in enumerate((B_A, B_B)):
                        dve.wait_ge(s[f"msg_mm{k}"], t.now)
                        if not t.first0:
                            dve.wait_ge(s["msg_done"], t.prev)
                            dve.wait_ge(s["uv_sl"], t.prev)
                        dve.tensor_tensor(msg_raw[:, 2 * k:2 * k + 2, :], pair(b), bias_pair(msg_bias),
                                          ALU.add).then_inc(s[f"msg_raw{k}"], 1)
                if t.layer0:
                    dve.wait_ge(s["hhd_done"], t.now)
                    if not t.first0:
                        dve.wait_ge(s["conv2_mm"], t.prev)
                    dve.tensor_tensor(hl[:, 1:3, :], h_diff[:], hh[:, 1:3, :].bitcast(F32),
                                      ALU.subtract).then_inc(s["hld_done"], 1)
                if t.layer1:
                    layer_norm_stats(t.prev, B_C[:], "yT_mm", stats, mv, var_eps, "", 4 * EPS)
                if t.layer1:
                    dve.wait_ge(s["rstd_done"], t.prev)
                    for c in range(C):
                        last = dve.tensor_scalar(x1[:, 1 - par, c, :], chunk(B_C, c), mv[:, c, 0:1], rstd[:, c:c + 1],
                                                 ALU.subtract, ALU.mult)
                    last.then_inc(s["x1_done"], 1)
                if t.layer0:
                    dve.wait_ge(s["shared_mm"], t.now)
                    if not t.first0:
                        dve.wait_ge(s["conv_sum_done"], t.prev)
                    dve.scalar_tensor_tensor(
                        out=by_parity(x_shared[:]),
                        in0=B_Z[:, 0:HALF].rearrange("p (e i) -> p e i", e=1).to_broadcast([P, 2, HALF]),
                        scalar=bn_scale[:, 1:2], in1=by_parity(xT[:, par, :]), op0=ALU.mult,
                        op1=ALU.add).then_inc(s["x_shared_done"], 1)
                if t.final:
                    dve.wait_ge(s["rden_done"], t.before)
                    dve.wait_ge(s["o_mm"], t.before)
                    for c in range(C):
                        last = dve.scalar_tensor_tensor(out=y2[:, c, :], in0=chunk(B_D, c), scalar=rden[:, c:c + 1],
                                                        in1=x1[:, par, c, :], op0=ALU.mult, op1=ALU.add)
                    last.then_inc(s["y2_done"], 1)
                if t.layer0:
                    dve.wait_ge(s["uv_mm"], t.now)
                    if not t.first0:
                        dve.wait_ge(s["dist_mm3"], t.prev)
                    dve.tensor_copy(U[:], B_A[0:KU, :]).then_inc(s["U_done"], 1)
                if t.layer1:
                    dve.wait_ge(s["x1h_done"], t.prev)
                    if not t.first1:
                        dve.wait_ge(s["z_mm1"], t.before)
                    dve.tensor_tensor(x1l[:], B_C[:], x1h[:].bitcast(F32), ALU.subtract).then_inc(s["x1l_done"], 1)
                if t.layer0:
                    mask_AT(0)
                if t.final:
                    layer_norm_stats(t.before, y2[:].rearrange("p c d -> p (c d)"), "y2_done", stats2, mv2, var_eps2, "2", EPS)
                if t.layer0:
                    mask_AT(1)
                if t.layer1:
                    for k, b in enumerate((B_C, B_D)):
                        dve.wait_ge(s[f"z_mm{k}"], t.prev)
                        if not t.first1:
                            dve.wait_ge(s["att_mm"], t.before)
                            dve.wait_ge(s["e_done3"], t.before)
                            dve.wait_ge(s["u_max_done"], t.before)
                        dve.tensor_tensor(z[:, 2 * k:2 * k + 2, :], pair(b), bias_pair(z_bias),
                                          ALU.add).then_inc(s[f"z_done{k}"], 1)
                    dve.wait_ge(s["z_done1"], t.prev)
                    if not t.first1:
                        dve.wait_ge(s["e_small3"], t.before)
                    dve.tensor_scalar(ai_small[:], z[:, :, AI], ALPHA, None, ALU.mult).then_inc(s["ai_small_done"], 1)
                if t.layer0:
                    mask_AT(2)
                if t.layer1:
                    for c in range(C):
                        dve.wait_ge(constants_ready, 1)
                        dve.wait_ge(s["ajb_mm"], t.prev)
                        dve.wait_ge(s["no_edge_done"], t.prev)
                        if not t.first1:
                            dve.wait_ge(s[f"e_done{c}"], t.before)
                            dve.wait_ge(s[f"e_small{c}"], t.before)
                            dve.wait_ge(s["u_max_done"], t.before)
                        dve.tensor_tensor_reduce(out=ajm[:, c, :], in0=no_edge[:, c, :], in1=B_C[:], scale=1.0,
                                                 scalar=-3.0e38, op0=ALU.add, op1=ALU.max,
                                                 accum_out=amax[:, c:c + 1]).then_inc(s[f"ajm_done{c}"], 1)
                if t.layer0:
                    mask_AT(3)
                if t.final:
                    dve.wait_ge(s["rstd2_done"], t.before)
                    dve.wait_ge(out_free, t.stored)
                    for c in range(C):
                        last = dve.tensor_scalar(out_sb[:, c, :], y2[:, c, :], mv2[:, c, 0:1], rstd2[:, c:c + 1],
                                                 ALU.subtract, ALU.mult)
                    last.then_inc(s["out_done"], 1)
                if t.layer0:
                    dve.wait_ge(s["conv2_mm"], t.now)
                    dve.wait_ge(s["x_shared_done"], t.now)
                    if not t.first0:
                        dve.wait_ge(s["xc_done"], t.prev)
                    dve.scalar_tensor_tensor(out=by_parity(conv_sum[:]),
                                             in0=B_CONV[:].rearrange("p (e i) -> p e i", e=2),
                                             scalar=bn_scale[:, 1:2], in1=by_parity(x_shared[:]), op0=ALU.mult,
                                             op1=ALU.add).then_inc(s["conv_sum_done"], 1)
                if t.layer1:
                    dve.wait_ge(s["ajm_done3"], t.prev)
                    dve.tensor_tensor(u_max[:], amax[:], z[:, :, AI], ALU.add).then_inc(s["u_max_done"], 1)
                    dve.wait_ge(s["u_max_done"], t.prev)
                    dve.scalar_tensor_tensor(out=leaky_max[:], in0=u_max[:], scalar=ALPHA, in1=u_max[:],
                                             op0=ALU.mult, op1=ALU.max).then_inc(s["leaky_max_done"], 1)
                    dve.wait_ge(s["leaky_max_done"], t.prev)
                    if not t.first1:
                        dve.wait_ge(s["p_done3"], t.before)
                    dve.tensor_scalar(neg_max[:], leaky_max[:], SINK, -1.0, ALU.max,
                                      ALU.mult).then_inc(s["neg_max_done"], 1)
                    dve.wait_ge(s["neg_max_done"], t.prev)
                    if not t.first1:
                        dve.wait_ge(s["sink_done"], t.before)
                    dve.tensor_scalar(sink_in[:], neg_max[:], SINK, None, ALU.add).then_inc(s["sink_in_done"], 1)

                def leaky(c):
                    dve.wait_ge(s[f"e_small{c}"], t.prev)
                    if not t.first1:
                        dve.wait_ge(s[f"p_done{c}"], t.before)
                    dve.scalar_tensor_tensor(out=e[:, c, :], in0=ajm[:, c, :], scalar=z[:, c, AI:AI + 1],
                                             in1=e_small[:, c, :], op0=ALU.add,
                                             op1=ALU.max).then_inc(s[f"e_done{c}"], 1)
                if t.layer1:
                    leaky(0)
                if t.layer0:
                    dve.wait_ge(s["xc_done"], t.now)
                    if not t.first0:
                        dve.wait_ge(s["conv_gates_mm"], t.prev)
                        dve.wait_ge(s["xcl_done"], t.prev)
                    dve.tensor_copy(xch[:], xc[:]).then_inc(s["xch_done"], 1)
                    dve.wait_ge(s["xch_done"], t.now)
                    dve.tensor_tensor(xcl[:], xc[:], xch[:].bitcast(F32), ALU.subtract).then_inc(s["xcl_done"], 1)
                if t.layer1:
                    leaky(1)
                if t.layer1:
                    leaky(2)
                    leaky(3)
                if t.layer0:
                    dve.wait_ge(s["xnh_done"], t.now)
                    if not t.first0:
                        dve.wait_ge(s["gates_mm"], t.prev)
                    dve.tensor_tensor(xnl[:], B_A[:], xnh[:].bitcast(F32), ALU.subtract).then_inc(s["xnl_done"], 1)
                if t.layer0:
                    dve.wait_ge(adj_loaded, t.loaded)
                    if t.layer1:
                        dve.wait_ge(s["ajm_done3"], t.prev)
                    dve.tensor_scalar(no_edge[:], adj_in[:], 0.0, MASKED, ALU.is_le,
                                      ALU.mult).then_inc(s["no_edge_done"], 1)

            def layer_norm_stats(when, src, ready, stats, mv, var_eps, tag, eps):
                dve.wait_ge(s[ready], when)
                for c in range(C):
                    last = dve.bn_stats(stats[:, c, :], src[:, c * P:(c + 1) * P])
                last.then_inc(s[f"stats{tag}_done"], 1)
                dve.wait_ge(constants_ready, 1)
                dve.wait_ge(s[f"stats{tag}_done"], when)
                for c in range(C):
                    last = dve.bn_aggr(mv[:, c, :], stats[:, c, :])
                last.then_inc(s[f"mv{tag}_done"], 1)
                dve.wait_ge(s[f"mv{tag}_done"], when)
                dve.tensor_scalar(var_eps[:], mv[:, :, 1], eps, None, ALU.add).then_inc(s[f"var{tag}_done"], 1)

            run_turns(dve, turn)

        @block.tensor
        def _(pe):
            def three(out, w, r, start, stop):
                pe.matmul(out, w[0], r[0], start=start, stop=False)
                pe.matmul(out, w[0], r[1], start=False, stop=False)
                return pe.matmul(out, w[1], r[0], start=False, stop=stop)

            def weight(k):
                return wh[:, k, :], wl[:, k, :]

            conv2_by_tap = raw_conv2[:].rearrange("p (i k) -> p i k", k=TAPS)
            raws = [raw_conv1[:]] + [raw_sums[:, a, :] for a in range(ODD)] + [conv2_by_tap[:, :, k] for k in range(TAPS)] \
                + [raw_ih[:, a, 0:D] for a in range(3)] + [raw_ih[:, a, D:2 * D] for a in range(3)] \
                + [raw_hh[:, a, :] for a in range(3)]
            pe.wait_ge(constants_ready, 1)
            pe.wait_ge(weights_loaded, 7 * 16)
            pe.wait_ge(params_loaded, 18 * 16)
            pe.transpose(B_C[:, 0:D], raw_msg[:], ident[:])
            pe.transpose(B_C[:, D:D + SE], raw_se[:], ident[0:SE, 0:SE])
            pe.transpose(B_C[:, 256:256 + D], raw_W[:], ident[:])
            pe.matmul(B_C[:, 256 + D:256 + D + 2], raw_W[:], att_w[:], start=True, stop=True)
            pe.matmul(B_D[:, 0:2], bW_col[:].to_broadcast([P, P]), att_w[:], start=True,
                      stop=True).then_inc(att_folded, 1)
            pe.wait_ge(taps_summed, 1)
            for k, raw in enumerate(raws):
                if k % C == 0 and k >= 4 * C:
                    pe.wait_ge(w_split, k // C - 3)
                last = pe.transpose(chunk(bank[(k // C) % 4], k % C), raw, ident[:])
                if k % C == C - 1 or k == len(raws) - 1:
                    last.then_inc(w_turned, 1)
            pe.wait_ge(w_split, -(-NW // C))
            pe.wait_ge(aug_copied, 7)

            CONVS = 3 * EVEN - 1
            X, XC, XN = (xh, xl), (xch, xcl), (xnh, xnl)

            def full(pr):
                return pr[0][:], pr[1][:]

            def turn(t):
                par = t.parity

                def conv2(first, end):
                    for k in range(first, end):
                        a, part = k % EVEN, k // EVEN
                        if k == EVEN:
                            pe.wait_ge(s["hld_done"], t.now)
                        w = ((CONV_SUM + a if a < ODD else CONV2 + TAPS - 1), CONV2 + 2 * a, CONV2 + 2 * a + 1)[part]
                        last = three((B_Z[:, 0:HALF], B_CONV[:, 0:HALF], B_CONV[:, HALF:N])[part], weight(w),
                                     (hh[:, part, a:a + HALF], hl[:, part, a:a + HALF]),
                                     a == 0, a == (EVEN, EVEN, ODD)[part] - 1)
                        if k == EVEN - 1:
                            last.then_inc(s["shared_mm"], 1)
                    if end == CONVS:
                        last.then_inc(s["conv2_mm"], 1)

                def dist_adj(c):
                    if c == 0:
                        pe.wait_ge(s["U_done"], t.now)
                        pe.wait_ge(s["V_done"], t.now)
                        pe.wait_ge(adj_loaded, t.loaded)
                    else:
                        pe.wait_ge(s[f"E_done{c - 1}"], t.now)
                    pe.matmul(B_A[:], U[:, c * P:(c + 1) * P], V[:], start=True, stop=True).then_inc(s[f"dist_mm{c}"], 1)
                    if c == 0:
                        pe.wait_ge(s["msg_raw1"], t.now)
                    elif c == 1:
                        if t.layer1:
                            pe.wait_ge(s["q2_done"], t.prev)
                    else:
                        pe.wait_ge(s[f"AT_done{c - 2}"], t.now)
                    for n in range(C):
                        last = pe.transpose(chunk((B_B, B_IN)[c % 2], n), adj_in[:, n, c * P:(c + 1) * P], ident[:])
                    last.then_inc(s[f"adjT_mm{c}"], 1)

                def p_turn(c):
                    b = B_D if c % 2 == 0 else B_C
                    pe.wait_ge(s[f"p_done{c}"], t.before)
                    if c >= 2:
                        pe.wait_ge(s[f"pT_done{c - 2}"], t.before)
                    for m in range(C):
                        last = pe.transpose(chunk(b, m), p[:, c, m * P:(m + 1) * P], ident[:])
                    last.then_inc(s[f"pT_mm{c}"], 1)

                if t.layer0:
                    pe.wait_ge(x_loaded, t.loaded)
                    if not t.first0:
                        pe.wait_ge(s["xnl_done"], t.prev)
                    for c in range(C):
                        last = pe.transpose(chunk(B_A, c), x_in[:, c, :], ident[:])
                    last.then_inc(s["xT_mm"], 1)
                if t.layer1:
                    pe.wait_ge(s["xnl_done"], t.prev)
                    for a, b in enumerate((B_R, B_Z, B_IN)):
                        last = three(b[:], weight(IH_MSG + a), full(XN), False, True)
                    last.then_inc(s["gates_mm"], 1)
                if t.final:
                    p_turn(0)
                    p_turn(1)
                if t.layer0:
                    pe.wait_ge(s["xl_done"], t.now)
                    if not t.first0:
                        pe.wait_ge(s["AT_done3"], t.prev)
                    three(B_B[:], weight(CONV1), full(X), True, True).then_inc(s["conv1_mm"], 1)
                    if t.layer1:
                        pe.wait_ge(s["ghb_done"], t.prev)
                    three(B_HN[:], weight(HH + 2), full(X), True, True).then_inc(s["hn_mm"], 1)
                if t.final:
                    p_turn(2)
                    p_turn(3)
                if t.layer0:
                    for k, b in enumerate((B_A, B_B)):
                        if k == 0:
                            pe.wait_ge(s["xh_done"], t.now)
                        else:
                            pe.wait_ge(s["h1_done"], t.now)
                        for c in (2 * k, 2 * k + 1):
                            last = three(pair(b)[:, c % 2, :], (chunk(xh, c), chunk(xl, c)),
                                         (msg_wh[:], msg_wl[:]), True, True)
                        last.then_inc(s[f"msg_mm{k}"], 1)
                    if t.layer1:
                        pe.wait_ge(s["tz_done"], t.prev)
                    pe.wait_ge(s["hlo_done"], t.now)
                    conv2(0, 4)
                if t.layer1:
                    pe.wait_ge(s["y_done"], t.prev)
                    if t.final:
                        pe.wait_ge(s["pT_done3"], t.before)
                    for c in range(C):
                        last = pe.transpose(chunk(B_C, c), y[:, c * P:(c + 1) * P], ident[:])
                    last.then_inc(s["yT_mm"], 1)
                if t.final:
                    pe.wait_ge(s["pT_done2"], t.before)
                    pe.wait_ge(s["pT_done3"], t.before)
                    for c in range(C):
                        last = pe.matmul(B_D[:], z[:, c, 0:D], pT[:, c, :], start=(c == 0), stop=(c == C - 1))
                    last.then_inc(s["att_mm"], 1)
                if t.layer0:
                    conv2(4, 9)
                if t.final:
                    pe.wait_ge(s["oT_done"], t.before)
                    for c in range(C):
                        last = pe.transpose(chunk(B_D, c), oT[:, c * P:(c + 1) * P], ident[:])
                    last.then_inc(s["o_mm"], 1)
                if t.layer0:
                    pe.wait_ge(constants_ready, 7)
                    pe.wait_ge(s["uv_done"], t.now)
                    pe.wait_ge(s["msg_raw0"], t.now)
                    for c in range(C):
                        last = pe.transpose(B_A[0:VOFF + KU, c * P:(c + 1) * P], uv[:, c, :], ident[:])
                    last.then_inc(s["uv_mm"], 1)
                    conv2(9, 11)
                if t.layer1:
                    pe.wait_ge(s["x1_done"], t.prev)
                    for c in range(C):
                        last = pe.transpose(chunk(B_C, c), x1[:, 1 - par, c, :], ident[:])
                    last.then_inc(s["x1T_mm"], 1)
                if t.layer0:
                    dist_adj(0)
                    conv2(11, 13)
                    dist_adj(1)
                    conv2(13, 15)
                if t.layer1:
                    pe.wait_ge(s["x1l_done"], t.prev)
                    if t.final:
                        pe.wait_ge(s["y2_done"], t.before)
                    for k, b in enumerate((B_C, B_D)):
                        for c in (2 * k, 2 * k + 1):
                            last = three(pair(b)[:, c % 2, :], (chunk(x1h, c), chunk(x1l, c)),
                                         (z_wh[:], z_wl[:]), True, True)
                        last.then_inc(s[f"z_mm{k}"], 1)
                if t.layer0:
                    dist_adj(2)
                    conv2(15, 17)
                if t.layer1:
                    pe.wait_ge(s["z_done1"], t.prev)
                    for c in range(C):
                        last = pe.transpose(chunk(B_C, c), z[:, c, AJ:AJ + 1].to_broadcast([P, P]), ident[:])
                    last.then_inc(s["ajb_mm"], 1)
                if t.layer0:
                    conv2(17, 19)
                    dist_adj(3)
                    conv2(19, CONVS)
                    pe.wait_ge(s["x_shared_done"], t.now)
                    three(B_Z[:], weight(HH + 1), full(X), True, False)
                    pe.wait_ge(s["msg_done"], t.now)
                    pe.wait_ge(s["AT_done3"], t.now)
                    for c in range(C):
                        last = pe.matmul(B_A[:], msg[:, c, :], AT[:, c, :], start=(c == 0), stop=(c == C - 1))
                    last.then_inc(s["nmp_mm"], 1)
                    pe.wait_ge(s["conv_sum_done"], t.now)
                    three(B_R[:], weight(HH), full(X), True, False).then_inc(s["xgates_mm"], 1)
                    pe.wait_ge(s["xcl_done"], t.now)
                    three(B_Z[:], weight(IH_CONV + 1), full(XC), False, False)
                    three(B_IN[:], weight(IH_CONV + 2), full(XC), True, False)
                    three(B_R[:], weight(IH_CONV), full(XC), False, False).then_inc(s["conv_gates_mm"], 1)

            run_turns(pe, turn)


_IN = ['x', 'adj', 'L0_gnn_w_se', 'L0_gnn_b_se', 'L0_gnn_conv1_w', 'L0_gnn_bn1_g', 'L0_gnn_bn1_b',
       'L0_gnn_bn1_m', 'L0_gnn_bn1_v', 'L0_gnn_conv2_w', 'L0_gnn_bn2_g', 'L0_gnn_bn2_b',
       'L0_gnn_bn2_m', 'L0_gnn_bn2_v', 'L0_gnn_w_msg', 'L0_gnn_b_msg', 'L0_gnn_w_ih', 'L0_gnn_b_ih',
       'L0_gnn_w_hh', 'L0_gnn_b_hh', 'L1_gnn_W', 'L1_gnn_bW', 'L1_gnn_wai', 'L1_gnn_bai',
       'L1_gnn_waj', 'L1_gnn_baj']


def kernel(**inputs):
    import numpy as _np
    import concourse.bacc as _bacc
    from concourse import mybir as _mybir
    from concourse.bass_utils import run_bass_kernel_spmd as _run

    nc = _bacc.Bacc("TRN2", target_bir_lowering=False, num_devices=1)
    arrays, args = {}, []
    for name in _IN:
        a = _np.ascontiguousarray(inputs[name])
        arrays[f"in_{name}_dram"] = a
        args.append(nc.dram_tensor(f"in_{name}_dram", a.shape, _mybir.dt.from_np(a.dtype),
                                   kind="ExternalInput").ap())
    out = nc.dram_tensor("out_dram", inputs["x"].shape, _mybir.dt.float32, kind="ExternalOutput").ap()
    resnorm_kernel(nc, *args, out)
    r = _run(nc, [arrays], core_ids=[0])
    return r.results[0]["out_dram"]
```

```python
import concourse.bass as bass
from concourse import mybir
from contextlib import ExitStack

F32 = mybir.dt.float32
F32R = mybir.dt.float32r
ALU = mybir.AluOpType
ACT = mybir.ActivationFunctionType


class Turn:

    def __init__(self, parity, before, prev, now, loaded, stored, layer0=True, layer1=True,
                 final=True, first0=False, first1=False):
        self.parity = parity
        self.now = now
        self.prev = prev
        self.before = before
        self.loaded = loaded
        self.stored = stored
        self.layer0, self.layer1, self.final = layer0, layer1, final
        self.first0 = first0
        self.first1 = first1


def resnorm_kernel(nc, x, adj, w_se, b_se, conv1_w, bn1_g, bn1_b, bn1_m, bn1_v, conv2_w, bn2_g,
                   bn2_b, bn2_m, bn2_v, w_msg, b_msg, w_ih, b_ih, w_hh, b_hh, W, bW, wai, bai,
                   waj, baj, out):
    G, N, D = x.shape
    P = 128
    C = N // P
    TAPS = conv2_w.shape[2]
    PAD = TAPS // 2
    SE = w_se.shape[0]
    AUG = D + 4
    KU = 4 * SE + 4
    VOFF = 32
    EPS = 1e-5
    ALPHA = 0.2
    SINK = -1e9
    MASKED = -9e15 / ALPHA

    ctx = ExitStack()
    with ctx:
        def sb(name, shape, dt=F32):
            return ctx.enter_context(nc.sbuf_tensor(name, shape, dt))

        def sem(name):
            return ctx.enter_context(nc.semaphore(name))

        ctx.enter_context(nc.allow_non_contiguous_dma("parameter vectors as columns, once"))

        ident = sb("ident", [P, P])
        three_col = sb("three_col", [P, 1])
        half_power = sb("half_power", [P, C])
        masked = sb("masked", [P, 2, C, N])
        no_edge, ajm = masked[:, 0, :, :], masked[:, 1, :, :]
        mask_words = masked[:].rearrange("p a c n -> p (a c n)")
        scores = sb("scores", [P, C, N])
        score_words = scores[:].rearrange("p c n -> p (c n)")
        EVEN, ODD = TAPS // 2 + 1, TAPS // 2
        raw_conv2 = mask_words[:, 0:D * TAPS]
        raw_sums = mask_words[:, D * TAPS:D * (TAPS + ODD)].rearrange("p (a o) -> p a o", a=ODD)
        raw_conv1, raw_msg, raw_W = (score_words[:, k * D:(k + 1) * D] for k in range(3))
        raw_se = score_words[0:SE, 3 * D:4 * D]
        raw_ih = score_words[:, 4 * D:10 * D].rearrange("p (a i) -> p a i", a=3)
        raw_hh = score_words[:, 10 * D:13 * D].rearrange("p (a i) -> p a i", a=3)
        NW = 1 + ODD + TAPS + 9
        wh = sb("wh", [P, NW, D], F32R)
        wl = sb("wl", [P, NW, D], F32R)
        CONV2, CONV1, HH = 0, TAPS, TAPS + 1
        IH_CONV, IH_MSG = TAPS + 4, TAPS + 7
        CONV_SUM = TAPS + 10
        msg_wh = sb("msg_wh", [P, AUG], F32R)
        msg_wl = sb("msg_wl", [P, AUG], F32R)
        z_wh = sb("z_wh", [P, AUG], F32R)
        z_wl = sb("z_wl", [P, AUG], F32R)
        aug_full = sb("aug_full", [P, 2, AUG])
        bn = sb("bn", [P, 8])
        bn_scale = sb("bn_scale", [P, 2])
        bn_shift = sb("bn_shift", [P, 2])
        bn_tmp = sb("bn_tmp", [P, 2])
        gru_bi = sb("gru_bi", [P, 3])
        gru_bh = sb("gru_bh", [P, 3])
        gru_half = sb("gru_half", [P, 3])
        msg_bias = sb("msg_bias", [P, AUG])
        z_bias = sb("z_bias", [P, AUG])
        att_w = sb("att_w", [P, 2])
        bW_col = sb("bW_col", [P, 1])
        att_b = sb("att_b", [P, 2])

        x_in = sb("x_in", [P, C, D])
        adj_in = sb("adj_in", [P, 2, C, N])
        xT = sb("xT", [P, 2, N])
        xh, xl = sb("xh", [P, N], F32R), sb("xl", [P, N], F32R)
        HALF = N // 2
        HW = HALF + PAD
        h1 = sb("h1", [P, N + 4])
        h_diff = sb("h_diff", [P, 2, HW])
        hh, hl = sb("hh", [P, 3, HW], F32R), sb("hl", [P, 3, HW], F32R)
        x_shared = sb("x_shared", [P, N])
        msg_raw = sb("msg_raw", [P, C, AUG])
        msg = sb("msg", [P, C, D])
        msgh, msgl = sb("msgh", [P, C, D], F32R), sb("msgl", [P, C, D], F32R)
        s_sq = sb("s_sq", [P, C, SE])
        sq_a, sq_b = sb("sq_a", [P, C, 1]), sb("sq_b", [P, C, 1])
        uv = sb("uv", [P, C, VOFF + KU])
        U, V = sb("U", [KU, N], F32R), sb("V", [KU, N], F32R)
        E = sb("E", [P, 2, N])
        AT = sb("AT", [P, 2, N])
        ATh, ATl = sb("ATh", [P, C, N], F32R), sb("ATl", [P, C, N], F32R)
        conv_sum = sb("conv_sum", [P, N])
        xc = sb("xc", [P, N])
        xch, xcl = sb("xch", [P, N], F32R), sb("xcl", [P, N], F32R)
        xnh, xnl = sb("xnh", [P, N], F32R), sb("xnl", [P, N], F32R)
        tz3 = sb("tz3", [P, N])
        tr, tz, ghb = sb("tr", [P, N]), sb("tz", [P, N]), sb("ghb", [P, N])
        q1, q2, nn = sb("q1", [P, N]), sb("q2", [P, N]), sb("nn", [P, N])
        n_part = nn
        x_part, y = sb("x_part", [P, N]), sb("y", [P, N])
        stats = sb("stats", [P, C, 6])
        mv = sb("mv", [P, C, 2])
        var_eps, rstd = sb("var_eps", [P, C]), sb("rstd", [P, C])
        x1 = sb("x1", [P, 2, C, D])
        x1h, x1l = sb("x1h", [P, N], F32R), sb("x1l", [P, N], F32R)
        z = sb("z", [P, C, AUG])
        zh, zl = sb("zh", [P, C, D], F32R), sb("zl", [P, C, D], F32R)
        AJ, AI = D, D + 1
        amax, u_max, leaky_max = sb("amax", [P, C]), sb("u_max", [P, C]), sb("leaky_max", [P, C])
        neg_max, sink_in, sink = sb("neg_max", [P, C]), sb("sink_in", [P, C]), sb("sink", [P, C])
        ai_small = sb("ai_small", [P, C])
        pTh, pTl = sb("pTh", [P, C, N], F32R), sb("pTl", [P, C, N], F32R)
        row_sum, den, rden = sb("row_sum", [P, C]), sb("den", [P, C]), sb("rden", [P, C])
        oT = sb("oT", [P, N])
        y2 = sb("y2", [P, C, D])
        stats2, mv2 = sb("stats2", [P, C, 6]), sb("mv2", [P, C, 2])
        var_eps2, rstd2 = sb("var_eps2", [P, C]), sb("rstd2", [P, C])
        out_sb = sb("out_sb", [P, C, D])

        bank = [ctx.enter_context(nc.psum_tensor(f"bank{k}", [P, N], F32)) for k in range(8)]
        B_CONV = B_R = bank[0]
        B_Z, B_IN, B_HN = bank[1], bank[2], bank[3]
        B_A, B_B = bank[4], bank[5]
        B_C, B_D = bank[6], bank[7]

        def chunk(ap, c, width=P):
            return ap[:, c * width:(c + 1) * width]

        WB = 6
        y2_row = y2[:].rearrange("p c d -> p (c d)")
        P_BANKS = (B_R, B_D, B_B, B_IN)

        def pair(b):
            return b[:, 0:2 * AUG].rearrange("p (c f) -> p c f", c=2)

        params_loaded, weights_loaded = sem("params_loaded"), sem("weights_loaded")
        conv2_loaded, late_params_loaded = sem("conv2_loaded"), sem("late_params_loaded")
        setup_pool, constants_ready = sem("setup_pool"), sem("constants_ready")
        w_turned, w_split, w_high = sem("w_turned"), sem("w_split"), sem("w_high")
        att_folded, aug_copied = sem("att_folded"), sem("aug_copied")
        setup_dve = sem("setup_dve")
        params_ready, taps_summed = sem("params_ready"), sem("taps_summed")
        x_loaded, adj_loaded, out_free = sem("x_loaded"), sem("adj_loaded"), sem("out_free")
        s = {n: sem(n) for n in (
            "xT_mm xT_done xh_done xl_done conv1_mm h1_done h_diff_done hho_done hlo_done hhd_done hld_done "
            "msg_mm0 msg_mm1 msg_raw0 msg_raw1 msg_done msgh_done msgl_done "
            "uv_sh uv_sl uv_squares uv_sum1 uv_sum uv_sqh uv_sql uv_done uv_mm U_done V_done "
            "dist_mm0 dist_mm1 dist_mm2 dist_mm3 adjT_mm0 adjT_mm1 adjT_mm2 adjT_mm3 "
            "E_done0 E_done1 E_done2 E_done3 AT_done0 AT_done1 AT_done2 AT_done3 ATh_done0 ATh_done1 ATh_done2 ATh_done3 ATl_done0 ATl_done1 ATl_done2 ATl_done3 "
            "no_edge_done shared_mm x_shared_done conv2_mm conv_sum_done xc_done xch_done xcl_done nmp_mm xnh_done xnl_done "
            "hn_mm xgates_mm conv_gates_mm gates_mm ghb_done tr_done tz_done q1_done q2_done "
            "nn_done tz3_done x_part_done n_part_done y_done "
            "yT_mm stats_done mv_done var_done rstd_done x1_done x1T_mm x1h_done x1l_done "
            "z_mm0 z_mm1 z_done0 z_done1 zh_done zl_done ajb_mm ai_small_done "
            "ajm_done0 ajm_done1 ajm_done2 ajm_done3 u_max_done leaky_max_done neg_max_done "
            "sink_in_done sink_done e_small0 e_small1 e_small2 e_small3 e_done0 e_done1 e_done2 "
            "e_done3 p_done0 p_done1 p_done2 p_done3 pT_mm0 pT_mm1 pT_mm2 pT_mm3 "
            "pTh_done0 pTh_done1 pTh_done2 pTh_done3 pTl_done0 pTl_done1 pTl_done2 pTl_done3 att_mm oT_done o_mm den_done rden_done "
            "y2_done stats2_done mv2_done var2_done rstd2_done out_done").split()}

        x_dram = x.rearrange("g (c p) d -> g p c d", p=P)
        adj_dram = adj.rearrange("g (c p) m -> g p c m", p=P)
        out_dram = out.rearrange("g (c p) d -> g p c d", p=P)

        def column(v):
            return v.rearrange("(p a) -> p a", a=1)

        def row_everywhere(v):
            return v.rearrange("(a n) -> a n", a=1).to_broadcast([P, v.shape[0]])

        def run_turns(eng, turn):
            turn(Turn(0, None, None, 1, 16, None, layer1=False, final=False, first0=True))
            turn(Turn(1, None, 1, 2, 32, None, final=False, first1=True))
            regs = {}
            for name in ("gm1", "g0", "g1", "g2", "s0", "s1", "s2", "s3"):
                regs[name] = eng.alloc_register(name)
            with eng.Fori(2, G, 2) as g:
                for k, name in enumerate(("gm1", "g0", "g1", "g2")):
                    eng.reg_add(regs[name], g, k - 1)
                for k in range(4):
                    eng.reg_mul(regs[f"s{k}"], regs[("gm1", "g0", "g1", "g2")[k]], 16)
                v = {name: eng.snap(r, min_val=1) for name, r in regs.items()}
                turn(Turn(0, v["gm1"], v["g0"], v["g1"], v["s2"], v["s0"]))
                turn(Turn(1, v["g0"], v["g1"], v["g2"], v["s3"], v["s1"]))
            turn(Turn(G % 2, G - 1, G, None, None, 16 * (G - 1), layer0=False))
            turn(Turn((G + 1) % 2, G, None, None, None, 16 * G, layer0=False, layer1=False))

        block = ctx.enter_context(nc.Block())

        @block.sync
        def _(sp):
            sp.dma_start(x_in[:], x_dram[0]).then_inc(x_loaded, 16)
            sp.dma_start(raw_conv2, conv2_w.rearrange("o i k -> o (i k)")).then_inc(conv2_loaded, 16)
            sp.dma_start(raw_conv1, conv1_w.rearrange("o i k -> o (i k)")).then_inc(weights_loaded, 16)
            sp.dma_start(raw_hh, w_hh.rearrange("(a o) i -> o a i", a=3)).then_inc(weights_loaded, 16)
            sp.dma_start(raw_ih, w_ih.rearrange("(a o) i -> o a i", a=3)).then_inc(weights_loaded, 16)
            sp.dma_start(raw_msg, w_msg).then_inc(weights_loaded, 16)
            sp.dma_start(raw_se, w_se).then_inc(weights_loaded, 16)
            sp.dma_start(raw_W, W).then_inc(weights_loaded, 16)
            for k, v in enumerate((bn1_g, bn1_b, bn1_m, bn1_v, bn2_g, bn2_b, bn2_m, bn2_v)):
                sp.dma_start(bn[:, k:k + 1], column(v)).then_inc(params_loaded, 16)
            sp.dma_start(gru_bi[:], b_ih.rearrange("(a p) -> p a", a=3)).then_inc(params_loaded, 16)
            sp.dma_start(gru_bh[:], b_hh.rearrange("(a p) -> p a", a=3)).then_inc(params_loaded, 16)
            sp.dma_start(adj_in[:, 0], adj_dram[0]).then_inc(adj_loaded, 16)

            def load_x(g, here):
                sp.wait_ge(s["xT_mm"], here)
                sp.dma_start(x_in[:], x_dram[g]).then_inc(x_loaded, 16)

            def load_adj(g, here, half, first=False):
                sp.wait_ge(s["adjT_mm0"], here)
                if not first:
                    sp.wait_ge(s["adjT_mm3"], here - 1)
                    sp.wait_ge(s["no_edge_done"], here - 1)
                sp.dma_start(adj_in[:, half], adj_dram[g]).then_inc(adj_loaded, 16)

            def store(g, here):
                sp.wait_ge(s["out_done"], here)
                sp.dma_start(out_dram[g], out_sb[:]).then_inc(out_free, 16)

            load_x(1, 1)
            load_adj(1, 1, 1, first=True)
            load_x(2, 2)
            load_adj(2, 2, 0)
            with sp.Fori(2, G - 2, 2) as g:
                for k in range(2):
                    load_x(g + k + 1, g + k + 1)
                    load_adj(g + k + 1, g + k + 1, (k + 1) % 2)
                    store(g + k - 2, g + k - 1)
            load_x(G - 1, G - 1)
            load_adj(G - 1, G - 1, (G - 1) % 2)
            store(G - 4, G - 3)
            store(G - 3, G - 2)
            store(G - 2, G - 1)
            store(G - 1, G)
            sp.wait_ge(out_free, 16 * (G + 1))

        @block.gpsimd
        def _(pool):
            pool.memset(ident[:], 0.0).then_inc(setup_pool, 1)
            pool.wait_ge(setup_pool, 1)
            pool.affine_select(out=ident[:], in_=ident[:], compare_op=ALU.not_equal, fill=1.0, base=0,
                               pattern=[[-1, P]], channel_multiplier=1).then_inc(constants_ready, 1)
            pool.dma_start(att_w[:, 0:1], waj.rearrange("a p -> p a")).then_inc(late_params_loaded, 16)
            pool.dma_start(att_w[:, 1:2], wai.rearrange("a p -> p a")).then_inc(late_params_loaded, 16)
            pool.dma_start(bW_col[:], column(bW)).then_inc(late_params_loaded, 16)
            pool.dma_start(att_b[:, 0:1], row_everywhere(baj)).then_inc(late_params_loaded, 16)
            pool.dma_start(att_b[:, 1:2], row_everywhere(bai)).then_inc(late_params_loaded, 16)
            pool.dma_start(msg_bias[:, 0:D], row_everywhere(b_msg)).then_inc(late_params_loaded, 16)
            pool.dma_start(msg_bias[:, D:D + SE], row_everywhere(b_se)).then_inc(late_params_loaded, 16)
            pool.dma_start(z_bias[:, 0:D], row_everywhere(bW)).then_inc(late_params_loaded, 16)
            pool.memset(half_power[:], -0.5).then_inc(constants_ready, 1)
            pool.memset(hh[:].bitcast(F32), 0.0).then_inc(constants_ready, 1)
            pool.memset(hl[:].bitcast(F32), 0.0).then_inc(constants_ready, 1)
            pool.memset(uv[:], 0.0).then_inc(constants_ready, 1)
            pool.memset(three_col[:], 3.0)
            pool.memset(h1[:], 0.0)
            pool.memset(h_diff[:], 0.0).then_inc(setup_pool, 1)
            pool.wait_ge(constants_ready, 5)
            pool.memset(uv[:, :, 4 * SE + 2:KU], 1.0).then_inc(constants_ready, 1)
            pool.memset(uv[:, :, VOFF + 4 * SE:VOFF + 4 * SE + 2], -1.0).then_inc(constants_ready, 1)
            bn4 = bn[:].rearrange("p (n k) -> p n k", n=2)
            pool.wait_ge(params_loaded, 10 * 16)
            pool.tensor_scalar(bn_tmp[:], bn4[:, :, 3], EPS, None, ALU.add).then_inc(setup_pool, 1)
            pool.tensor_tensor(gru_half[:, 0:2], gru_bi[:, 0:2], gru_bh[:, 0:2], ALU.add)
            pool.tensor_copy(gru_half[:, 2:3], gru_bh[:, 2:3]).then_inc(setup_pool, 1)
            pool.wait_ge(constants_ready, 2)
            pool.wait_ge(setup_pool, 3)
            pool.tensor_tensor(bn_scale[:], bn_tmp[:], half_power[:, 0:2], ALU.pow).then_inc(setup_pool, 1)
            pool.wait_ge(setup_pool, 4)
            pool.tensor_scalar(gru_half[:], gru_half[:], 0.5, None, ALU.mult).then_inc(setup_pool, 1)
            pool.wait_ge(setup_pool, 5)
            pool.tensor_tensor(bn_scale[:], bn_scale[:], bn4[:, :, 0], ALU.mult).then_inc(setup_pool, 1)
            pool.wait_ge(setup_pool, 7)
            pool.tensor_tensor(bn_tmp[:], bn_scale[:], bn4[:, :, 2], ALU.mult).then_inc(setup_pool, 1)
            pool.wait_ge(setup_pool, 8)
            pool.tensor_tensor(bn_shift[:], bn4[:, :, 1], bn_tmp[:], ALU.subtract).then_inc(params_ready, 1)

            def turn(t):
                par = t.parity

                def h_difference():
                    pool.wait_ge(s["h1_done"], t.now)
                    if t.first0:
                        pool.wait_ge(setup_pool, 2)
                    else:
                        pool.wait_ge(s["hhd_done"], t.prev)
                        pool.wait_ge(s["hld_done"], t.prev)
                    pool.tensor_tensor(h_diff[:, 0, PAD // 2:PAD // 2 + HALF], h1[:, 2:2 + N:2],
                                       h1[:, 3:3 + N:2], ALU.subtract)
                    pool.tensor_tensor(h_diff[:, 1, PAD // 2 - 1:PAD // 2 + HALF], h1[:, 2:4 + N:2],
                                       h1[:, 1:3 + N:2], ALU.subtract).then_inc(s["h_diff_done"], 1)

                def x_times():
                    pool.wait_ge(s["tz3_done"], t.prev)
                    if not t.first1:
                        pool.wait_ge(s["y_done"], t.before)
                    pool.tensor_tensor(x_part[:], tz3[:], xT[:, 1 - par, :], ALU.mult).then_inc(s["x_part_done"], 1)

                def distance_columns():
                    def u_view(a):
                        return uv[:, :, 2 * SE * a:2 * SE * (a + 1)].rearrange("p c (b k) -> p c b k", b=2)

                    def v_view(a):
                        return uv[:, :, VOFF:VOFF + 4 * SE].rearrange("p c (b a k) -> p c b a k", b=2, a=2)[:, :, :, a, :]

                    sv = msg_raw[:, :, D:D + SE]

                    def twice(ap):
                        return ap.rearrange("p c (b k) -> p c b k", b=1).to_broadcast([P, C, 2, SE])

                    uq = uv[:, :, 4 * SE:4 * SE + 1]
                    pool.wait_ge(constants_ready, 7)
                    pool.wait_ge(s["msg_raw1"], t.now)
                    pool.wait_ge(s["msg_raw0"], t.now)
                    if not t.first0:
                        pool.wait_ge(s["uv_mm"], t.prev)
                    pool.tensor_copy(u_view(0).bitcast(F32R), twice(sv)).then_inc(s["uv_sh"], 1)
                    pool.tensor_tensor(s_sq[:], sv, sv, ALU.mult).then_inc(s["uv_squares"], 1)
                    pool.wait_ge(s["uv_sh"], t.now)
                    pool.tensor_tensor(u_view(1).bitcast(F32R), twice(sv), u_view(0),
                                       ALU.subtract).then_inc(s["uv_sl"], 1)
                    pool.wait_ge(s["uv_squares"], t.now)
                    pool.tensor_tensor(sq_a[:], s_sq[:, :, 0:1], s_sq[:, :, 1:2],
                                       ALU.add).then_inc(s["uv_sum1"], 1)
                    pool.wait_ge(constants_ready, 7)
                    pool.wait_ge(s["uv_sl"], t.now)
                    pool.tensor_scalar(v_view(0), u_view(0), 2.0, None, ALU.mult)
                    pool.tensor_scalar(v_view(1), u_view(1), 2.0, None, ALU.mult)
                    pool.wait_ge(s["uv_sum1"], t.now)
                    pool.tensor_tensor(sq_b[:], sq_a[:], s_sq[:, :, 2:3], ALU.add).then_inc(s["uv_sum"], 1)
                    pool.wait_ge(constants_ready, 7)
                    pool.wait_ge(s["uv_sum"], t.now)
                    pool.tensor_copy(uq.bitcast(F32R), sq_b[:]).then_inc(s["uv_sqh"], 1)
                    pool.wait_ge(s["uv_sqh"], t.now)
                    pool.tensor_tensor(uv[:, :, 4 * SE + 1:4 * SE + 2].bitcast(F32R), sq_b[:], uq,
                                       ALU.subtract).then_inc(s["uv_sql"], 1)
                    pool.wait_ge(constants_ready, 7)
                    pool.wait_ge(s["uv_sql"], t.now)
                    pool.tensor_scalar(uv[:, :, VOFF + 4 * SE + 2:VOFF + KU],
                                       uv[:, :, 4 * SE:4 * SE + 2], -1.0, None,
                                       ALU.mult).then_inc(s["uv_done"], 1)

                def AT_low(c):
                    pool.wait_ge(s[f"ATh_done{c}"], t.now)
                    if not t.first0:
                        pool.wait_ge(s["nmp_mm"], t.prev)
                    pool.tensor_tensor(ATl[:, c, :], AT[:, c % 2, :], ATh[:, c, :].bitcast(F32),
                                       ALU.subtract).then_inc(s[f"ATl_done{c}"], 1)

                def layer_norm_power():
                    pool.wait_ge(s["var_done"], t.prev)
                    pool.tensor_tensor(rstd[:], var_eps[:], half_power[:], ALU.pow).then_inc(s["rstd_done"], 1)

                def message_low():
                    pool.wait_ge(s["msgh_done"], t.now)
                    if not t.first0:
                        pool.wait_ge(s["nmp_mm"], t.prev)
                    pool.tensor_tensor(msgl[:], msg[:], msgh[:].bitcast(F32), ALU.subtract).then_inc(s["msgl_done"], 1)

                def output_power():
                    pool.wait_ge(s["var2_done"], t.before)
                    pool.tensor_tensor(rstd2[:], var_eps2[:], half_power[:], ALU.pow).then_inc(s["rstd2_done"], 1)

                def z_low():
                    pool.wait_ge(s["zh_done"], t.prev)
                    if not t.first1:
                        pool.wait_ge(s["att_mm"], t.before)
                    pool.tensor_tensor(zl[:], z[:, :, 0:D], zh[:].bitcast(F32), ALU.subtract).then_inc(s["zl_done"], 1)

                def output():
                    pool.wait_ge(constants_ready, 1)
                    pool.wait_ge(s["rstd2_done"], t.before)
                    pool.wait_ge(out_free, t.stored)
                    for c in range(C):
                        last = pool.tensor_scalar(out_sb[:, c, :], y2[:, c, :], mv2[:, c, 0:1], rstd2[:, c:c + 1],
                                                 ALU.subtract, ALU.mult)
                    last.then_inc(s["out_done"], 1)

                if not t.layer0:
                    if t.layer1:
                        x_times()
                        layer_norm_power()
                    if t.final:
                        output_power()
                    if t.layer1:
                        z_low()
                        output()
                    return
                if t.layer0:
                    h_difference()
                if t.layer1:
                    x_times()
                if t.layer0:
                    distance_columns()
                    message_low()
                if t.layer1:
                    layer_norm_power()
                if t.layer0:
                    AT_low(0)
                    AT_low(1)
                    AT_low(2)
                    AT_low(3)
                if t.layer1:
                    z_low()
                if t.final:
                    output_power()
                    output()

            run_turns(pool, turn)

        @block.scalar
        def _(act):
            def turn(t):
                par = t.parity

                def exp_dist(c):
                    act.wait_ge(s[f"dist_mm{c}"], t.now)
                    if c >= 2:
                        act.wait_ge(s[f"AT_done{c - 2}"], t.now)
                    elif not t.first0:
                        act.wait_ge(s[f"AT_done{c + 2}"], t.prev)
                    act.activation(E[:, c % 2, :], B_A[:], ACT.Exp).then_inc(s[f"E_done{c}"], 1)

                def p_out(c):
                    act.wait_ge(s[f"pT_mm{c}"], t.before)
                    act.activation(pTh[:, :, c * P:(c + 1) * P],
                                   P_BANKS[c][:].rearrange("p (m n) -> p m n", m=C),
                                   ACT.Copy).then_inc(s[f"pTh_done{c}"], 1)

                def AT_high(c):
                    act.wait_ge(s[f"AT_done{c}"], t.now)
                    if not t.first0:
                        act.wait_ge(s["nmp_mm"], t.prev)
                    act.activation(ATh[:, c, :], AT[:, c % 2, :], ACT.Copy).then_inc(s[f"ATh_done{c}"], 1)

                def x_out():
                    act.wait_ge(s["xT_mm"], t.now)
                    if t.layer1 and not t.first1:
                        act.wait_ge(s["x_part_done"], t.before)
                    act.activation(xT[:, par, :], B_A[:], ACT.Copy).then_inc(s["xT_done"], 1)
                    if not t.first0:
                        act.wait_ge(s["xgates_mm"], t.prev)
                        act.wait_ge(s["xl_done"], t.prev)
                    act.activation(xh[:], B_A[:], ACT.Copy).then_inc(s["xh_done"], 1)

                def hidden_n():
                    act.wait_ge(s["hn_mm"], t.now)
                    act.wait_ge(params_ready, 1)
                    if not t.first0:
                        act.wait_ge(s["q1_done"], t.prev)
                    act.activation(ghb[:], B_HN[:], ACT.Identity, bias=gru_half[:, 2:3],
                                   scale=0.5).then_inc(s["ghb_done"], 1)

                def r_gate():
                    act.wait_ge(s["gates_mm"], t.prev)
                    if not t.first1:
                        act.wait_ge(s["q1_done"], t.before)
                    act.activation(tr[:], B_R[:], ACT.Tanh, bias=gru_half[:, 0:1], scale=0.5).then_inc(s["tr_done"], 1)

                def z_gate():
                    act.wait_ge(s["gates_mm"], t.prev)
                    if not t.first1:
                        act.wait_ge(s["n_part_done"], t.before)
                    act.activation(tz[:], B_Z[:], ACT.Tanh, bias=gru_half[:, 1:2], scale=0.5).then_inc(s["tz_done"], 1)
                    act.wait_ge(s["tz_done"], t.prev)
                    if not t.first1:
                        act.wait_ge(s["x_part_done"], t.before)
                    act.activation(tz3[:], tz[:], ACT.Identity, bias=three_col[:]).then_inc(s["tz3_done"], 1)

                def h_out():
                    act.wait_ge(s["conv1_mm"], t.now)
                    act.wait_ge(params_ready, 1)
                    if t.first0:
                        act.wait_ge(setup_pool, 2)
                    else:
                        act.wait_ge(s["hlo_done"], t.prev)
                        act.wait_ge(s["h_diff_done"], t.prev)
                    act.activation(h1[:, 2:2 + N], B_B[:], ACT.Relu, bias=bn_shift[:, 0:1],
                                   scale=bn_scale[:, 0:1]).then_inc(s["h1_done"], 1)

                def h_odd_high():
                    act.wait_ge(s["h1_done"], t.now)
                    if t.first0:
                        act.wait_ge(constants_ready, 4)
                    else:
                        act.wait_ge(s["conv2_mm"], t.prev)
                    act.activation(hh[:, 0, PAD // 2:PAD // 2 + HALF], h1[:, 3:3 + N:2],
                                   ACT.Copy).then_inc(s["hho_done"], 1)

                def n_gate():
                    act.wait_ge(s["q2_done"], t.prev)
                    if not t.first1:
                        act.wait_ge(s["n_part_done"], t.before)
                    act.activation(nn[:], q2[:], ACT.Tanh, bias=gru_bi[:, 2:3]).then_inc(s["nn_done"], 1)

                def h_difference_high():
                    act.wait_ge(s["h_diff_done"], t.now)
                    if not t.first0:
                        act.wait_ge(s["conv2_mm"], t.prev)
                        act.wait_ge(s["hld_done"], t.prev)
                    act.activation(hh[:, 1:3, :], h_diff[:], ACT.Copy).then_inc(s["hhd_done"], 1)

                def message():
                    act.wait_ge(s["msg_raw0"], t.now)
                    act.wait_ge(s["msg_raw1"], t.now)
                    if not t.first0:
                        act.wait_ge(s["msgl_done"], t.prev)
                    act.activation(msg[:], msg_raw[:, :, 0:D], ACT.Relu).then_inc(s["msg_done"], 1)
                    act.wait_ge(s["msg_done"], t.now)
                    if not t.first0:
                        act.wait_ge(s["nmp_mm"], t.prev)
                    act.activation(msgh[:], msg[:], ACT.Copy).then_inc(s["msgh_done"], 1)

                def attention_out():
                    act.wait_ge(s["att_mm"], t.before)
                    act.activation(oT[:], B_HN[:], ACT.Copy).then_inc(s["oT_done"], 1)

                def V_out():
                    act.wait_ge(s["uv_mm"], t.now)
                    if not t.first0:
                        act.wait_ge(s["dist_mm3"], t.prev)
                    act.activation(V[:], B_A[VOFF:VOFF + KU, :], ACT.Copy).then_inc(s["V_done"], 1)

                def x1_high():
                    act.wait_ge(s["x1T_mm"], t.prev)
                    if not t.first1:
                        act.wait_ge(s["z_mm1"], t.before)
                    act.activation(x1h[:], B_C[:], ACT.Copy).then_inc(s["x1h_done"], 1)

                def z_high():
                    act.wait_ge(s["z_done1"], t.prev)
                    if not t.first1:
                        act.wait_ge(s["att_mm"], t.before)
                        act.wait_ge(s["zl_done"], t.before)
                    act.activation(zh[:], z[:, :, 0:D], ACT.Copy).then_inc(s["zh_done"], 1)

                def small_slope(c):
                    act.wait_ge(s[f"ajm_done{c}"], t.prev)
                    act.wait_ge(s["ai_small_done"], t.prev)
                    if not t.first1:
                        act.wait_ge(s[f"pT_mm{c}"], t.before)
                    act.activation(scores[:, c, :], ajm[:, c, :], ACT.Identity, bias=ai_small[:, c:c + 1],
                                   scale=ALPHA).then_inc(s[f"e_small{c}"], 1)

                def conv_relu():
                    act.wait_ge(s["conv_sum_done"], t.now)
                    if not t.first0:
                        act.wait_ge(s["xcl_done"], t.prev)
                    act.activation(xc[:], conv_sum[:], ACT.Relu, bias=bn_shift[:, 1:2]).then_inc(s["xc_done"], 1)

                def sink_exp():
                    act.wait_ge(s["sink_in_done"], t.prev)
                    if not t.first1:
                        act.wait_ge(s["den_done"], t.before)
                    act.activation(sink[:], sink_in[:], ACT.Exp).then_inc(s["sink_done"], 1)

                def exp_scores(c, when):
                    act.wait_ge(s[f"e_done{c}"], when)
                    act.wait_ge(s["neg_max_done"], when)
                    act.activation(scores[:, c, :], scores[:, c, :], ACT.Exp, bias=neg_max[:, c:c + 1],
                                   accum_out=row_sum[:, c:c + 1]).then_inc(s[f"p_done{c}"], 1)

                def aggregate_high():
                    act.wait_ge(s["nmp_mm"], t.now)
                    if not t.first0:
                        act.wait_ge(s["gates_mm"], t.prev)
                    act.activation(xnh[:], B_A[:], ACT.Copy).then_inc(s["xnh_done"], 1)

                if not t.layer0:
                    if t.final:
                        exp_scores(2, t.before)
                        exp_scores(3, t.before)
                    if t.layer1:
                        r_gate()
                        z_gate()
                    if t.final:
                        p_out(0)
                    if t.layer1:
                        n_gate()
                    if t.final:
                        p_out(1)
                        p_out(2)
                        p_out(3)
                    if t.layer1:
                        x1_high()
                    if t.final:
                        attention_out()
                    if t.layer1:
                        small_slope(0)
                        small_slope(1)
                        small_slope(2)
                        small_slope(3)
                        z_high()
                        sink_exp()
                        exp_scores(0, t.prev)
                        exp_scores(1, t.prev)
                    return
                if t.layer0:
                    x_out()
                if t.final:
                    exp_scores(2, t.before)
                    exp_scores(3, t.before)
                if t.layer1:
                    r_gate()
                if t.layer0:
                    h_out()
                    h_odd_high()
                if t.layer1:
                    z_gate()
                if t.final:
                    p_out(0)
                if t.layer1:
                    n_gate()
                if t.layer0:
                    h_difference_high()
                if t.final:
                    p_out(1)
                if t.layer0:
                    message()
                    V_out()
                if t.final:
                    p_out(2)
                    p_out(3)
                if t.layer0:
                    exp_dist(0)
                if t.layer1:
                    x1_high()
                if t.layer0:
                    exp_dist(1)
                    AT_high(0)
                    AT_high(1)
                    exp_dist(2)
                    exp_dist(3)
                    AT_high(2)
                if t.layer1:
                    small_slope(0)
                if t.final:
                    attention_out()
                if t.layer1:
                    z_high()
                if t.layer0:
                    AT_high(3)
                    conv_relu()
                if t.layer1:
                    small_slope(1)
                if t.layer0:
                    aggregate_high()
                if t.layer1:
                    small_slope(2)
                    small_slope(3)
                    sink_exp()
                    exp_scores(0, t.prev)
                    exp_scores(1, t.prev)
                if t.layer0:
                    hidden_n()

            for k in range(0, NW, C):
                n = min(C, NW - k)
                act.wait_ge(w_turned, k // C + 1)
                act.activation(wh[:, k:k + n, :], bank[(k // C) % WB][:, 0:n * P].rearrange("p (w o) -> p w o", w=n),
                               ACT.Copy).then_inc(w_high, 1)
            act.wait_ge(att_folded, 1)
            act.wait_ge(setup_dve, 1)
            act.activation(aug_full[:, 0, 0:D + SE], B_C[:, 0:D + SE], ACT.Copy).then_inc(aug_copied, 1)
            act.activation(aug_full[:, 1, 0:D + 2], B_C[:, 256:256 + D + 2], ACT.Copy).then_inc(aug_copied, 1)
            act.wait_ge(aug_copied, 2)
            act.activation(msg_wh[:], aug_full[:, 0, :], ACT.Copy).then_inc(aug_copied, 1)
            act.activation(z_wh[:], aug_full[:, 1, :], ACT.Copy).then_inc(aug_copied, 1)
            act.wait_ge(params_loaded, 10 * 16)
            run_turns(act, turn)

        @block.vector
        def _(dve):
            dve.memset(msg_bias[:, D + SE:AUG], 0.0).then_inc(out_free, 16)
            dve.memset(z_bias[:, D + 2:AUG], 0.0)
            dve.memset(aug_full[:], 0.0).then_inc(setup_dve, 1)
            dve.wait_ge(conv2_loaded, 16)
            taps = raw_conv2.rearrange("p (i k) -> p k i", k=TAPS)
            dve.tensor_tensor(raw_sums, taps[:, 0:2 * ODD:2, :], taps[:, 1:2 * ODD:2, :],
                               ALU.add).then_inc(taps_summed, 1)
            for k in range(0, NW, C):
                n = min(C, NW - k)
                dve.wait_ge(w_turned, k // C + 1)
                dve.wait_ge(w_high, k // C + 1)
                dve.tensor_tensor(wl[:, k:k + n, :], bank[(k // C) % WB][:, 0:n * P].rearrange("p (w o) -> p w o", w=n),
                                  wh[:, k:k + n, :].bitcast(F32), ALU.subtract).then_inc(w_split, 1)
            dve.wait_ge(att_folded, 1)
            dve.wait_ge(late_params_loaded, 8 * 16)
            dve.tensor_tensor(z_bias[:, D:D + 2], B_D[:, 0:2], att_b[:], ALU.add).then_inc(setup_dve, 1)
            dve.wait_ge(aug_copied, 4)
            dve.tensor_tensor(msg_wl[:], aug_full[:, 0, :], msg_wh[:].bitcast(F32),
                              ALU.subtract).then_inc(aug_copied, 1)
            dve.tensor_tensor(z_wl[:], aug_full[:, 1, :], z_wh[:].bitcast(F32),
                              ALU.subtract).then_inc(aug_copied, 1)
            dve.wait_ge(setup_dve, 2)

            def by_parity(ap):
                return ap.rearrange("p (i e) -> p e i", e=2)

            def bias_pair(b):
                return b[:].rearrange("p (c f) -> p c f", c=1).to_broadcast([P, 2, AUG])

            def turn(t):
                par = t.parity

                def mask_AT(c):
                    dve.wait_ge(s[f"E_done{c}"], t.now)
                    dve.wait_ge(s[f"adjT_mm{c}"], t.now)
                    if c >= 2:
                        dve.wait_ge(s[f"ATh_done{c - 2}"], t.now)
                        dve.wait_ge(s[f"ATl_done{c - 2}"], t.now)
                    elif not t.first0:
                        dve.wait_ge(s[f"ATh_done{c + 2}"], t.prev)
                        dve.wait_ge(s[f"ATl_done{c + 2}"], t.prev)
                    dve.tensor_tensor(AT[:, c % 2, :], E[:, c % 2, :], (B_B, B_IN)[c % 2][:],
                                      ALU.mult).then_inc(s[f"AT_done{c}"], 1)

                def p_out(c):
                    dve.wait_ge(s[f"pT_mm{c}"], t.before)
                    dve.wait_ge(s[f"pTh_done{c}"], t.before)
                    here = pTh[:, :, c * P:(c + 1) * P]
                    dve.tensor_tensor(pTl[:, :, c * P:(c + 1) * P],
                                      P_BANKS[c][:].rearrange("p (m n) -> p m n", m=C), here.bitcast(F32),
                                      ALU.subtract).then_inc(s[f"pTl_done{c}"], 1)

                def x_low():
                    dve.wait_ge(s["xh_done"], t.now)
                    dve.wait_ge(s["xT_done"], t.now)
                    if not t.first0:
                        dve.wait_ge(s["xgates_mm"], t.prev)
                    dve.tensor_tensor(xl[:], xT[:, par, :], xh[:].bitcast(F32),
                                      ALU.subtract).then_inc(s["xl_done"], 1)

                def denominator():
                    if not t.layer1:
                        dve.wait_ge(s["out_done"], G - 1)
                    else:
                        dve.wait_ge(s["no_edge_done"], t.prev)
                    dve.wait_ge(s["sink_done"], t.before)
                    dve.wait_ge(s["p_done3"], t.before)
                    dve.tensor_tensor(den[:], row_sum[:], sink[:], ALU.add).then_inc(s["den_done"], 1)
                    dve.wait_ge(s["den_done"], t.before)
                    dve.reciprocal(rden[:], den[:]).then_inc(s["rden_done"], 1)

                def n_hidden():
                    dve.wait_ge(s["tr_done"], t.prev)
                    dve.wait_ge(s["ghb_done"], t.prev)
                    if not t.first1:
                        dve.wait_ge(s["q2_done"], t.before)
                    dve.scalar_tensor_tensor(out=q1[:], in0=tr[:], scalar=1.0, in1=ghb[:], op0=ALU.add,
                                             op1=ALU.mult).then_inc(s["q1_done"], 1)

                def n_sum():
                    dve.wait_ge(s["q1_done"], t.prev)
                    if not t.first1:
                        dve.wait_ge(s["nn_done"], t.before)
                    dve.tensor_tensor(q2[:], q1[:], B_IN[:], ALU.add).then_inc(s["q2_done"], 1)

                def h_odd_low():
                    body = slice(PAD // 2, PAD // 2 + HALF)
                    dve.wait_ge(s["hho_done"], t.now)
                    if not t.first0:
                        dve.wait_ge(s["conv2_mm"], t.prev)
                    dve.tensor_tensor(hl[:, 0, body], h1[:, 3:3 + N:2], hh[:, 0, body].bitcast(F32),
                                      ALU.subtract).then_inc(s["hlo_done"], 1)

                def n_times():
                    dve.wait_ge(s["nn_done"], t.prev)
                    dve.wait_ge(s["tz_done"], t.prev)
                    if not t.first1:
                        dve.wait_ge(s["y_done"], t.before)
                    dve.scalar_tensor_tensor(out=n_part[:], in0=tz[:], scalar=-1.0, in1=nn[:], op0=ALU.add,
                                             op1=ALU.mult).then_inc(s["n_part_done"], 1)

                def y_sum():
                    dve.wait_ge(s["n_part_done"], t.prev)
                    dve.wait_ge(s["x_part_done"], t.prev)
                    if not t.first1:
                        dve.wait_ge(s["yT_mm"], t.before)
                    dve.tensor_tensor(y[:], x_part[:], n_part[:], ALU.subtract).then_inc(s["y_done"], 1)

                def messages(k):
                    dve.wait_ge(s[f"msg_mm{k}"], t.now)
                    if not t.first0:
                        dve.wait_ge(s["msg_done"], t.prev)
                        dve.wait_ge(s["uv_sl"], t.prev)
                    dve.tensor_tensor(msg_raw[:, 2 * k:2 * k + 2, :], pair((B_A, B_B)[k]), bias_pair(msg_bias),
                                      ALU.add).then_inc(s[f"msg_raw{k}"], 1)

                def h_difference_low():
                    dve.wait_ge(s["hhd_done"], t.now)
                    if not t.first0:
                        dve.wait_ge(s["conv2_mm"], t.prev)
                    dve.tensor_tensor(hl[:, 1:3, :], h_diff[:], hh[:, 1:3, :].bitcast(F32),
                                      ALU.subtract).then_inc(s["hld_done"], 1)

                def U_out():
                    dve.wait_ge(s["uv_mm"], t.now)
                    if not t.first0:
                        dve.wait_ge(s["dist_mm3"], t.prev)
                    dve.tensor_copy(U[:], B_A[0:KU, :]).then_inc(s["U_done"], 1)

                def normalise():
                    dve.wait_ge(s["rstd_done"], t.prev)
                    for c in range(C):
                        last = dve.tensor_scalar(x1[:, 1 - par, c, :], chunk(B_C, c), mv[:, c, 0:1], rstd[:, c:c + 1],
                                                 ALU.subtract, ALU.mult)
                    last.then_inc(s["x1_done"], 1)

                def shared_sum():
                    dve.wait_ge(s["shared_mm"], t.now)
                    if t.first0:
                        dve.wait_ge(params_ready, 1)
                    if not t.first0:
                        dve.wait_ge(s["conv_sum_done"], t.prev)
                    dve.scalar_tensor_tensor(
                        out=by_parity(x_shared[:]),
                        in0=B_Z[:, 0:HALF].rearrange("p (e i) -> p e i", e=1).to_broadcast([P, 2, HALF]),
                        scalar=bn_scale[:, 1:2], in1=by_parity(xT[:, par, :]), op0=ALU.mult,
                        op1=ALU.add).then_inc(s["x_shared_done"], 1)

                def second_sum():
                    dve.wait_ge(s["rden_done"], t.before)
                    dve.wait_ge(s["o_mm"], t.before)
                    for c in range(C):
                        last = dve.scalar_tensor_tensor(out=y2[:, c, :], in0=chunk(B_HN, c), scalar=rden[:, c:c + 1],
                                                        in1=x1[:, par, c, :], op0=ALU.mult, op1=ALU.add)
                    last.then_inc(s["y2_done"], 1)

                def x1_low():
                    dve.wait_ge(s["x1h_done"], t.prev)
                    if not t.first1:
                        dve.wait_ge(s["z_mm1"], t.before)
                    dve.tensor_tensor(x1l[:], B_C[:], x1h[:].bitcast(F32), ALU.subtract).then_inc(s["x1l_done"], 1)

                def z_sum():
                    for k, b in enumerate((B_C, B_D)):
                        dve.wait_ge(s[f"z_mm{k}"], t.prev)
                        if not t.first1:
                            dve.wait_ge(s["zl_done"], t.before)
                            dve.wait_ge(s["zh_done"], t.before)
                            dve.wait_ge(s["e_done3"], t.before)
                            dve.wait_ge(s["u_max_done"], t.before)
                        dve.tensor_tensor(z[:, 2 * k:2 * k + 2, :], pair(b), bias_pair(z_bias),
                                          ALU.add).then_inc(s[f"z_done{k}"], 1)
                    dve.wait_ge(s["z_done1"], t.prev)
                    if not t.first1:
                        dve.wait_ge(s["e_small3"], t.before)
                    dve.tensor_scalar(ai_small[:], z[:, :, AI], ALPHA, None, ALU.mult).then_inc(s["ai_small_done"], 1)

                def edges(c):
                    dve.wait_ge(constants_ready, 1)
                    dve.wait_ge(s["ajb_mm"], t.prev)
                    dve.wait_ge(s["no_edge_done"], t.prev)
                    if not t.first1:
                        dve.wait_ge(s[f"e_done{c}"], t.before)
                        dve.wait_ge(s[f"e_small{c}"], t.before)
                        dve.wait_ge(s["u_max_done"], t.before)
                    dve.tensor_tensor_reduce(out=ajm[:, c, :], in0=no_edge[:, c, :], in1=B_C[:], scale=1.0,
                                             scalar=-3.0e38, op0=ALU.add, op1=ALU.max,
                                             accum_out=amax[:, c:c + 1]).then_inc(s[f"ajm_done{c}"], 1)

                def conv_sum_up():
                    dve.wait_ge(s["conv2_mm"], t.now)
                    dve.wait_ge(s["x_shared_done"], t.now)
                    if not t.first0:
                        dve.wait_ge(s["xc_done"], t.prev)
                    dve.scalar_tensor_tensor(out=by_parity(conv_sum[:]),
                                             in0=B_CONV[:].rearrange("p (e i) -> p e i", e=2),
                                             scalar=bn_scale[:, 1:2], in1=by_parity(x_shared[:]), op0=ALU.mult,
                                             op1=ALU.add).then_inc(s["conv_sum_done"], 1)

                def row_max():
                    dve.wait_ge(s["ajm_done3"], t.prev)
                    dve.tensor_tensor(u_max[:], amax[:], z[:, :, AI], ALU.add).then_inc(s["u_max_done"], 1)

                def conv_high():
                    dve.wait_ge(s["xc_done"], t.now)
                    if not t.first0:
                        dve.wait_ge(s["conv_gates_mm"], t.prev)
                        dve.wait_ge(s["xcl_done"], t.prev)
                    dve.tensor_copy(xch[:], xc[:]).then_inc(s["xch_done"], 1)

                def row_leaky():
                    dve.wait_ge(s["u_max_done"], t.prev)
                    dve.scalar_tensor_tensor(out=leaky_max[:], in0=u_max[:], scalar=ALPHA, in1=u_max[:],
                                             op0=ALU.mult, op1=ALU.max).then_inc(s["leaky_max_done"], 1)

                def conv_low():
                    dve.wait_ge(s["xch_done"], t.now)
                    dve.tensor_tensor(xcl[:], xc[:], xch[:].bitcast(F32), ALU.subtract).then_inc(s["xcl_done"], 1)

                def row_negative():
                    dve.wait_ge(s["leaky_max_done"], t.prev)
                    if not t.first1:
                        dve.wait_ge(s["p_done3"], t.before)
                    dve.tensor_scalar(neg_max[:], leaky_max[:], SINK, -1.0, ALU.max,
                                      ALU.mult).then_inc(s["neg_max_done"], 1)
                    dve.wait_ge(s["neg_max_done"], t.prev)
                    if not t.first1:
                        dve.wait_ge(s["sink_done"], t.before)
                    dve.tensor_scalar(sink_in[:], neg_max[:], SINK, None, ALU.add).then_inc(s["sink_in_done"], 1)

                def leaky(c, when):
                    dve.wait_ge(s[f"e_small{c}"], when)
                    dve.scalar_tensor_tensor(out=scores[:, c, :], in0=ajm[:, c, :], scalar=z[:, c, AI:AI + 1],
                                             in1=scores[:, c, :], op0=ALU.add,
                                             op1=ALU.max).then_inc(s[f"e_done{c}"], 1)

                def aggregate_low():
                    dve.wait_ge(s["xnh_done"], t.now)
                    if not t.first0:
                        dve.wait_ge(s["gates_mm"], t.prev)
                    dve.tensor_tensor(xnl[:], B_A[:], xnh[:].bitcast(F32), ALU.subtract).then_inc(s["xnl_done"], 1)

                def edge_mask():
                    dve.wait_ge(s["adjT_mm3"], t.prev)
                    if not t.first1:
                        dve.wait_ge(s["ajm_done3"], t.before)
                    dve.tensor_scalar(no_edge, adj_in[:, 1 - par], 0.0, MASKED, ALU.is_le,
                                      ALU.mult).then_inc(s["no_edge_done"], 1)

                def last_output():
                    if t.layer1:
                        return
                    dve.wait_ge(s["rstd2_done"], t.before)
                    dve.wait_ge(out_free, t.stored)
                    for c in range(C):
                        last = dve.tensor_scalar(out_sb[:, c, :], y2[:, c, :], mv2[:, c, 0:1], rstd2[:, c:c + 1],
                                                 ALU.subtract, ALU.mult)
                    last.then_inc(s["out_done"], 1)

                if not t.layer0:
                    if t.final:
                        leaky(3, t.before)
                    if t.layer1:
                        edge_mask()
                        n_hidden()
                        n_sum()
                    if t.final:
                        p_out(0)
                    if t.layer1:
                        n_times()
                        y_sum()
                    if t.final:
                        p_out(1)
                        p_out(2)
                    if t.layer1:
                        layer_norm_stats(t.prev, B_C[:], "yT_mm", stats, "")
                    if t.final:
                        p_out(3)
                    if t.layer1:
                        layer_norm_var(t.prev, stats, mv, var_eps, "", 4 * EPS)
                    if t.final:
                        denominator()
                    if t.layer1:
                        normalise()
                        x1_low()
                        z_sum()
                    if t.final:
                        second_sum()
                    if t.layer1:
                        edges(0)
                    if t.final:
                        layer_norm_stats(t.before, y2_row, "y2_done", stats2, "2")
                        layer_norm_var(t.before, stats2, mv2, var_eps2, "2", EPS)
                        last_output()
                    if t.layer1:
                        edges(1)
                        edges(2)
                        edges(3)
                        row_max()
                        row_leaky()
                        row_negative()
                        leaky(0, t.prev)
                        leaky(1, t.prev)
                        leaky(2, t.prev)
                    return
                if t.final:
                    leaky(3, t.before)
                if t.layer0:
                    x_low()
                if t.layer1:
                    edge_mask()
                    n_hidden()
                if t.layer0:
                    messages(0)
                    h_odd_low()
                if t.layer1:
                    n_sum()
                if t.layer0:
                    messages(1)
                if t.final:
                    p_out(0)
                if t.layer1:
                    n_times()
                    y_sum()
                if t.layer0:
                    h_difference_low()
                if t.final:
                    p_out(1)
                if t.layer1:
                    layer_norm_stats(t.prev, B_C[:], "yT_mm", stats, "")
                    layer_norm_var(t.prev, stats, mv, var_eps, "", 4 * EPS)
                if t.layer0:
                    U_out()
                if t.final:
                    p_out(2)
                if t.layer1:
                    normalise()
                if t.final:
                    p_out(3)
                if t.layer0:
                    mask_AT(0)
                if t.layer1:
                    x1_low()
                if t.layer0:
                    mask_AT(1)
                    shared_sum()
                if t.layer1:
                    z_sum()
                    edges(0)
                if t.layer0:
                    mask_AT(2)
                if t.final:
                    denominator()
                if t.layer1:
                    edges(1)
                    edges(2)
                    edges(3)
                if t.layer0:
                    mask_AT(3)
                if t.layer1:
                    row_max()
                    row_leaky()
                if t.layer0:
                    conv_sum_up()
                if t.final:
                    second_sum()
                if t.layer1:
                    row_negative()
                if t.layer0:
                    conv_high()
                if t.layer1:
                    leaky(0, t.prev)
                if t.layer0:
                    conv_low()
                if t.layer1:
                    leaky(1, t.prev)
                if t.final:
                    layer_norm_stats(t.before, y2_row, "y2_done", stats2, "2")
                    layer_norm_var(t.before, stats2, mv2, var_eps2, "2", EPS)
                if t.layer0:
                    aggregate_low()
                if t.layer1:
                    leaky(2, t.prev)

            def layer_norm_stats(when, src, ready, stats, tag):
                dve.wait_ge(s[ready], when)
                for c in range(C):
                    last = dve.bn_stats(stats[:, c, :], src[:, c * P:(c + 1) * P])
                last.then_inc(s[f"stats{tag}_done"], 1)

            def layer_norm_var(when, stats, mv, var_eps, tag, eps):
                dve.wait_ge(constants_ready, 1)
                dve.wait_ge(s[f"stats{tag}_done"], when)
                for c in range(C):
                    last = dve.bn_aggr(mv[:, c, :], stats[:, c, :])
                last.then_inc(s[f"mv{tag}_done"], 1)
                dve.wait_ge(s[f"mv{tag}_done"], when)
                dve.tensor_scalar(var_eps[:], mv[:, :, 1], eps, None, ALU.add).then_inc(s[f"var{tag}_done"], 1)

            run_turns(dve, turn)

        @block.tensor
        def _(pe):
            def three(out, w, r, start, stop):
                pe.matmul(out, w[0], r[0], start=start, stop=False)
                pe.matmul(out, w[0], r[1], start=False, stop=False)
                return pe.matmul(out, w[1], r[0], start=False, stop=stop)

            def weight(k):
                return wh[:, k, :], wl[:, k, :]

            conv2_by_tap = raw_conv2.rearrange("p (i k) -> p i k", k=TAPS)
            raws = [conv2_by_tap[:, :, k] for k in range(TAPS)] + [raw_conv1] \
                + [raw_hh[:, a, :] for a in range(3)] \
                + [raw_ih[:, a, 0:D] for a in range(3)] + [raw_ih[:, a, D:2 * D] for a in range(3)] \
                + [raw_sums[:, a, :] for a in range(ODD)]
            pe.wait_ge(constants_ready, 1)
            pe.wait_ge(conv2_loaded, 16)
            for k, raw in enumerate(raws):
                if k == CONV1:
                    pe.wait_ge(weights_loaded, 6 * 16)
                if k == CONV_SUM:
                    pe.wait_ge(taps_summed, 1)
                if k % C == 0 and k >= WB * C:
                    pe.wait_ge(w_split, k // C - WB + 1)
                last = pe.transpose(chunk(bank[(k // C) % WB], k % C), raw, ident[:])
                if k % C == C - 1 or k == len(raws) - 1:
                    last.then_inc(w_turned, 1)
            pe.wait_ge(late_params_loaded, 8 * 16)
            pe.transpose(B_C[:, 0:D], raw_msg, ident[:])
            pe.transpose(B_C[:, D:D + SE], raw_se, ident[0:SE, 0:SE])
            pe.transpose(B_C[:, 256:256 + D], raw_W, ident[:])
            pe.matmul(B_C[:, 256 + D:256 + D + 2], raw_W, att_w[:], start=True, stop=True)
            pe.matmul(B_D[:, 0:2], bW_col[:].to_broadcast([P, P]), att_w[:], start=True,
                      stop=True).then_inc(att_folded, 1)
            pe.wait_ge(w_split, WB)


            CONVS = 3 * EVEN - 1
            X, XC, XN = (xh, xl), (xch, xcl), (xnh, xnl)

            def full(pr):
                return pr[0][:], pr[1][:]

            def turn(t):
                par = t.parity

                def conv2(first, end):
                    for k in range(first, end):
                        a, part = k % EVEN, k // EVEN
                        if k == 0:
                            pe.wait_ge(s["hlo_done"], t.now)
                            if t.layer1:
                                pe.wait_ge(s["tz_done"], t.prev)
                        if k == EVEN:
                            pe.wait_ge(s["hld_done"], t.now)
                            if t.final:
                                pe.wait_ge(s["pTl_done0"], t.before)
                        w = ((CONV_SUM + a if a < ODD else CONV2 + TAPS - 1), CONV2 + 2 * a, CONV2 + 2 * a + 1)[part]
                        last = three((B_Z[:, 0:HALF], B_CONV[:, 0:HALF], B_CONV[:, HALF:N])[part], weight(w),
                                     (hh[:, part, a:a + HALF], hl[:, part, a:a + HALF]),
                                     a == 0, a == (EVEN, EVEN, ODD)[part] - 1)
                        if k == EVEN - 1:
                            last.then_inc(s["shared_mm"], 1)
                    if end == CONVS:
                        last.then_inc(s["conv2_mm"], 1)

                def dist_adj(c):
                    if c == 0:
                        pe.wait_ge(s["U_done"], t.now)
                        pe.wait_ge(s["V_done"], t.now)
                        pe.wait_ge(adj_loaded, t.loaded)
                    else:
                        pe.wait_ge(s[f"E_done{c - 1}"], t.now)
                    pe.matmul(B_A[:], U[:, c * P:(c + 1) * P], V[:], start=True, stop=True).then_inc(s[f"dist_mm{c}"], 1)
                    if c == 0:
                        pe.wait_ge(s["msg_raw1"], t.now)
                        if t.final:
                            pe.wait_ge(s["pTl_done2"], t.before)
                    elif c == 1:
                        if t.layer1:
                            pe.wait_ge(s["q2_done"], t.prev)
                        if t.final:
                            pe.wait_ge(s["pTl_done3"], t.before)
                    else:
                        pe.wait_ge(s[f"AT_done{c - 2}"], t.now)
                    for n in range(C):
                        last = pe.transpose(chunk((B_B, B_IN)[c % 2], n), adj_in[:, par, n, c * P:(c + 1) * P], ident[:])
                    last.then_inc(s[f"adjT_mm{c}"], 1)

                def message(k):
                    pe.wait_ge(s[("xh_done", "h1_done")[k]], t.now)
                    for c in (2 * k, 2 * k + 1):
                        last = three(pair((B_A, B_B)[k])[:, c % 2, :], (chunk(xh, c), chunk(xl, c)),
                                     (msg_wh[:], msg_wl[:]), True, True)
                    last.then_inc(s[f"msg_mm{k}"], 1)

                def p_turn(c):
                    b = B_D if c % 2 == 0 else B_C
                    pe.wait_ge(s[f"p_done{c}"], t.before)
                    if c >= 2:
                        pe.wait_ge(s[f"pTl_done{c - 2}"], t.before)
                    for m in range(C):
                        last = pe.transpose(chunk(b, m), scores[:, c, m * P:(m + 1) * P], ident[:])
                    last.then_inc(s[f"pT_mm{c}"], 1)

                def x_turn():
                    pe.wait_ge(x_loaded, t.loaded)
                    if not t.first0:
                        pe.wait_ge(s["xnl_done"], t.prev)
                    for c in range(C):
                        last = pe.transpose(chunk(B_A, c), x_in[:, c, :], ident[:])
                    last.then_inc(s["xT_mm"], 1)

                def gates():
                    pe.wait_ge(s["xnl_done"], t.prev)
                    for a, b in enumerate((B_R, B_Z, B_IN)):
                        last = three(b[:], weight(IH_MSG + a), full(XN), False, True)
                    last.then_inc(s["gates_mm"], 1)

                def conv1():
                    pe.wait_ge(s["xl_done"], t.now)
                    if t.first0:
                        pe.wait_ge(w_split, -(-NW // C))
                        pe.wait_ge(aug_copied, 6)
                    else:
                        pe.wait_ge(s["AT_done3"], t.prev)
                    three(B_B[:], weight(CONV1), full(X), True, True).then_inc(s["conv1_mm"], 1)

                def y_turn():
                    pe.wait_ge(s["y_done"], t.prev)
                    for c in range(C):
                        last = pe.transpose(chunk(B_C, c), y[:, c * P:(c + 1) * P], ident[:])
                    last.then_inc(s["yT_mm"], 1)

                def p_turn(c):
                    pe.wait_ge(s[f"p_done{c}"], t.before)
                    if t.layer0 and c == 2:
                        pe.wait_ge(s["msg_raw1"], t.now)
                    if t.layer1 and c in (0, 3):
                        pe.wait_ge(s["tr_done" if c == 0 else "q2_done"], t.prev)
                    for m in range(C):
                        last = pe.transpose(chunk(P_BANKS[c], m), scores[:, c, m * P:(m + 1) * P], ident[:])
                    last.then_inc(s[f"pT_mm{c}"], 1)

                def uv_turn():
                    pe.wait_ge(constants_ready, 7)
                    pe.wait_ge(s["uv_done"], t.now)
                    pe.wait_ge(s["msg_raw0"], t.now)
                    for c in range(C):
                        last = pe.transpose(B_A[0:VOFF + KU, c * P:(c + 1) * P], uv[:, c, :], ident[:])
                    last.then_inc(s["uv_mm"], 1)

                def x1_turn():
                    pe.wait_ge(s["x1_done"], t.prev)
                    for c in range(C):
                        last = pe.transpose(chunk(B_C, c), x1[:, 1 - par, c, :], ident[:])
                    last.then_inc(s["x1T_mm"], 1)

                def attention():
                    for c in range(C):
                        pe.wait_ge(s[f"pTl_done{c}"], t.before)
                    pe.wait_ge(s["zl_done"], t.before)
                    if t.layer1:
                        pe.wait_ge(s["ghb_done"], t.prev)
                    for c in range(C):
                        last = three(B_HN[:], (zh[:, c, :], zl[:, c, :]), (pTh[:, c, :], pTl[:, c, :]),
                                     c == 0, c == C - 1)
                    last.then_inc(s["att_mm"], 1)

                def attention_turn():
                    pe.wait_ge(s["oT_done"], t.before)
                    for c in range(C):
                        last = pe.transpose(chunk(B_HN, c), oT[:, c * P:(c + 1) * P], ident[:])
                    last.then_inc(s["o_mm"], 1)

                def z_product():
                    pe.wait_ge(s["x1l_done"], t.prev)
                    for k, b in enumerate((B_C, B_D)):
                        if k == 1 and t.final:
                            pe.wait_ge(s["pTl_done1"], t.before)
                        for c in (2 * k, 2 * k + 1):
                            last = three(pair(b)[:, c % 2, :], (chunk(x1h, c), chunk(x1l, c)),
                                         (z_wh[:], z_wl[:]), True, True)
                        last.then_inc(s[f"z_mm{k}"], 1)

                def aj_everywhere():
                    pe.wait_ge(s["z_done1"], t.prev)
                    for c in range(C):
                        last = pe.transpose(chunk(B_C, c), z[:, c, AJ:AJ + 1].to_broadcast([P, P]), ident[:])
                    last.then_inc(s["ajb_mm"], 1)

                def x_gates():
                    if t.final:
                        pe.wait_ge(s["y2_done"], t.before)
                    if t.layer1:
                        pe.wait_ge(s["ghb_done"], t.prev)
                    three(B_HN[:], weight(HH + 2), full(X), True, True).then_inc(s["hn_mm"], 1)
                    pe.wait_ge(s["x_shared_done"], t.now)
                    three(B_Z[:], weight(HH + 1), full(X), True, False)

                def x_gate_r():
                    pe.wait_ge(s["conv_sum_done"], t.now)
                    three(B_R[:], weight(HH), full(X), True, False).then_inc(s["xgates_mm"], 1)

                def aggregate():
                    pe.wait_ge(s["E_done3"], t.now)
                    pe.wait_ge(s["msgl_done"], t.now)
                    for c in range(C):
                        pe.wait_ge(s[f"ATh_done{c}"], t.now)
                        pe.wait_ge(s[f"ATl_done{c}"], t.now)
                        last = three(B_A[:], (msgh[:, c, :], msgl[:, c, :]), (ATh[:, c, :], ATl[:, c, :]),
                                     c == 0, c == C - 1)
                    last.then_inc(s["nmp_mm"], 1)

                def conv_gates():
                    pe.wait_ge(s["xcl_done"], t.now)
                    three(B_Z[:], weight(IH_CONV + 1), full(XC), False, False)
                    three(B_IN[:], weight(IH_CONV + 2), full(XC), True, False)
                    three(B_R[:], weight(IH_CONV), full(XC), False, False).then_inc(s["conv_gates_mm"], 1)

                if not t.layer0:
                    if t.layer1:
                        gates()
                    if t.final:
                        p_turn(0)
                        p_turn(1)
                        p_turn(2)
                        p_turn(3)
                    if t.layer1:
                        y_turn()
                    if t.final:
                        attention()
                    if t.layer1:
                        x1_turn()
                        z_product()
                    if t.final:
                        attention_turn()
                    if t.layer1:
                        aj_everywhere()
                    return
                if t.layer0:
                    x_turn()
                if t.layer1:
                    gates()
                if t.layer0:
                    conv1()
                    message(0)
                if t.final:
                    p_turn(0)
                    p_turn(1)
                if t.layer0:
                    message(1)
                    conv2(0, 9)
                if t.final:
                    p_turn(2)
                    p_turn(3)
                if t.layer1:
                    y_turn()
                if t.layer0:
                    conv2(9, 11)
                    uv_turn()
                    conv2(11, 18)
                    dist_adj(0)
                    conv2(18, 20)
                if t.layer1:
                    x1_turn()
                if t.layer0:
                    conv2(20, 21)
                    dist_adj(1)
                    conv2(21, 23)
                if t.layer1:
                    z_product()
                if t.layer0:
                    dist_adj(2)
                if t.layer1:
                    aj_everywhere()
                if t.layer0:
                    dist_adj(3)
                if t.final:
                    attention()
                if t.layer0:
                    conv2(23, CONVS)
                if t.final:
                    attention_turn()
                if t.layer0:
                    aggregate()
                    x_gate_r()
                    x_gates()
                    conv_gates()

            run_turns(pe, turn)


_IN = ['x', 'adj', 'L0_gnn_w_se', 'L0_gnn_b_se', 'L0_gnn_conv1_w', 'L0_gnn_bn1_g', 'L0_gnn_bn1_b',
       'L0_gnn_bn1_m', 'L0_gnn_bn1_v', 'L0_gnn_conv2_w', 'L0_gnn_bn2_g', 'L0_gnn_bn2_b',
       'L0_gnn_bn2_m', 'L0_gnn_bn2_v', 'L0_gnn_w_msg', 'L0_gnn_b_msg', 'L0_gnn_w_ih', 'L0_gnn_b_ih',
       'L0_gnn_w_hh', 'L0_gnn_b_hh', 'L1_gnn_W', 'L1_gnn_bW', 'L1_gnn_wai', 'L1_gnn_bai',
       'L1_gnn_waj', 'L1_gnn_baj']


def kernel(**inputs):
    import numpy as _np
    import concourse.bacc as _bacc
    from concourse import mybir as _mybir
    from concourse.bass_utils import run_bass_kernel_spmd as _run

    nc = _bacc.Bacc("TRN2", target_bir_lowering=False, num_devices=1)
    arrays, args = {}, []
    for name in _IN:
        a = _np.ascontiguousarray(inputs[name])
        arrays[f"in_{name}_dram"] = a
        args.append(nc.dram_tensor(f"in_{name}_dram", a.shape, _mybir.dt.from_np(a.dtype),
                                   kind="ExternalInput").ap())
    out = nc.dram_tensor("out_dram", inputs["x"].shape, _mybir.dt.float32, kind="ExternalOutput").ap()
    resnorm_kernel(nc, *args, out)
    r = _run(nc, [arrays], core_ids=[0])
    return r.results[0]["out_dram"]
```
